# Optimizing a Trainium2 kernel written in Bass

```python
import numpy as np
import jax
import jax.numpy as jnp

def _softmax(x, axis=-1):
    return jax.nn.softmax(x, axis=axis)

def _gelu(x):
    return jax.nn.gelu(x, approximate=True)

def _silu(x):
    return jax.nn.silu(x)

def _sigmoid(x):
    return jax.nn.sigmoid(x)

def _layernorm(x, axis=-1, eps=1e-05):
    m = jnp.mean(x, axis=axis, keepdims=True)
    v = jnp.var(x, axis=axis, keepdims=True)
    return (x - m) / jnp.sqrt(v + eps)

def _scatter_add(tgt, idx, src, axis=0):
    return tgt.at[idx].add(src)

def _segment_sum(src, seg, n):
    return jax.ops.segment_sum(src, seg, n)
kernel_name = 'mk_adaln_d1_jaxref_r8_e6a3db'

def setup_inputs(seed: int=0):
    np.random.seed(seed)
    _w = jnp.asarray

    def _L0_attn_setup():
        import jax, jax.numpy as jnp
        import numpy as np
        D_MODEL = 256
        D_STATE = 64
        D_CONV = 4
        EXPAND = 2
        HEADDIM = 128
        NGROUPS = 1
        CHUNK = 32
        D_INNER = EXPAND * D_MODEL
        NHEADS = D_INNER // HEADDIM
        CONV_DIM = D_INNER + 2 * NGROUPS * D_STATE
        D_IN_PROJ = 2 * D_INNER + 2 * NGROUPS * D_STATE + NHEADS
        BATCH = 2
        SEQLEN = 512
        LN_EPS = 1e-05

        def segsum(x):
            T = x.shape[-1]
            xe = jnp.broadcast_to(x[..., None], (*x.shape, T))
            strict_lower = jnp.tril(jnp.ones((T, T), bool), -1)
            xe = jnp.where(strict_lower, xe, 0.0)
            s = jnp.cumsum(xe, axis=-2)
            lower = jnp.tril(jnp.ones((T, T), bool), 0)
            return jnp.where(lower, s, -jnp.inf)

        def ssd_minimal_discrete(X, A, B, C, block_len):
            b, length = (X.shape[0], X.shape[1])
            pad = -length % block_len
            if pad:
                padt = lambda t: jnp.pad(t, [(0, 0), (0, pad)] + [(0, 0)] * (t.ndim - 2))
                X, A, B, C = (padt(X), padt(A), padt(B), padt(C))
            c = (length + pad) // block_len
            X = X.reshape(b, c, block_len, NHEADS, HEADDIM)
            B = B.reshape(b, c, block_len, NHEADS, D_STATE)
            C = C.reshape(b, c, block_len, NHEADS, D_STATE)
            A = A.reshape(b, c, block_len, NHEADS).transpose(0, 3, 1, 2)
            A_cumsum = jnp.cumsum(A, axis=-1)
            L = jnp.exp(segsum(A))
            Y_diag = jnp.einsum('bclhn,bcshn,bhcls,bcshp->bclhp', C, B, L, X)
            decay_states = jnp.exp(A_cumsum[:, :, :, -1:] - A_cumsum)
            states = jnp.einsum('bclhn,bhcl,bclhp->bchpn', B, decay_states, X)
            init = jnp.zeros_like(states[:, :1])
            states = jnp.concatenate([init, states], axis=1)
            A_last = jnp.pad(A_cumsum[:, :, :, -1], ((0, 0), (0, 0), (1, 0)))
            decay_chunk = jnp.exp(segsum(A_last))
            new_states = jnp.einsum('bhzc,bchpn->bzhpn', decay_chunk, states)
            states = new_states[:, :-1]
            state_decay_out = jnp.exp(A_cumsum)
            Y_off = jnp.einsum('bclhn,bchpn,bhcl->bclhp', C, states, state_decay_out)
            Y = (Y_diag + Y_off).reshape(b, c * block_len, NHEADS, HEADDIM)
            return Y[:, :length]
        key = jax.random.key(seed)
        ks = jax.random.split(key, 12)
        u = jax.random.normal(ks[0], (BATCH, SEQLEN, D_MODEL), jnp.float32)
        s_in = 1.0 / np.sqrt(D_MODEL)
        in_proj_w = jax.random.normal(ks[1], (D_IN_PROJ, D_MODEL), jnp.float32) * s_in
        in_proj_b = jax.random.normal(ks[2], (D_IN_PROJ,), jnp.float32) * 0.01
        conv_w = jax.random.normal(ks[3], (CONV_DIM, 1, D_CONV), jnp.float32) * 0.5
        conv_b = jax.random.normal(ks[4], (CONV_DIM,), jnp.float32) * 0.01
        dt = jnp.exp(jax.random.uniform(ks[5], (NHEADS,)) * (np.log(0.1) - np.log(0.001)) + np.log(0.001))
        dt = jnp.clip(dt, 0.0001, None)
        dt_bias = dt + jnp.log(-jnp.expm1(-dt))
        A_log = jnp.log(jax.random.uniform(ks[6], (NHEADS,), minval=1.0, maxval=16.0))
        ln_w = jnp.ones((D_INNER,), jnp.float32)
        ln_b = jnp.zeros((D_INNER,), jnp.float32)
        out_proj_w = jax.random.normal(ks[7], (D_MODEL, D_INNER), jnp.float32) / np.sqrt(D_INNER)
        out_proj_b = jax.random.normal(ks[8], (D_MODEL,), jnp.float32) * 0.01
        return {'u': u, 'in_proj_w': in_proj_w, 'in_proj_b': in_proj_b, 'conv_w': conv_w, 'conv_b': conv_b, 'dt_bias': dt_bias, 'A_log': A_log, 'ln_w': ln_w, 'ln_b': ln_b, 'out_proj_w': out_proj_w, 'out_proj_b': out_proj_b}
    _L0_attn_in = _L0_attn_setup()

    def _L0_ffn_setup():
        import jax, jax.numpy as jnp
        import numpy as np
        B, S, D, F, E, K = (2, 256, 256, 512, 8, 1)

        def _silu_mul(gu):
            g, u = jnp.split(gu, 2, axis=-1)
            return jax.nn.silu(g) * u

        def _moe_forward(hidden_states, router_w, w_gate_up, w_down, shared_gate_up, shared_down, top_k=K):
            b, s, d = hidden_states.shape
            x = hidden_states.reshape(-1, d)
            router_logits = x @ router_w.T
            topk_vals, topk_ids = jax.lax.top_k(router_logits, top_k)
            gate = jax.nn.sigmoid(topk_vals.astype(jnp.float32)).astype(x.dtype)
            xs = (x[:, None, :] * gate[:, :, None]).reshape(-1, d)
            ids_flat = topk_ids.reshape(-1)
            n_experts = w_gate_up.shape[0]

            def body(acc, inp):
                wg, wd, e = inp
                h = _silu_mul(xs @ wg)
                o = h @ wd
                mask = (ids_flat == e)[:, None]
                return (acc + jnp.where(mask, o, jnp.zeros((), o.dtype)), None)
            acc0 = jnp.zeros_like(xs)
            routed, _ = jax.lax.scan(body, acc0, (w_gate_up, w_down, jnp.arange(n_experts)))
            routed = routed.reshape(-1, top_k, d).sum(1)
            shared = _silu_mul(x @ shared_gate_up) @ shared_down
            return (routed + shared).reshape(b, s, d)
        key = jax.random.key(seed)
        ks = jax.random.split(key, 6)
        scale = 0.02
        return {'hidden_states': jax.random.normal(ks[0], (B, S, D), jnp.float32), 'router_w': jax.random.normal(ks[1], (E, D), jnp.float32) * scale, 'w_gate_up': jax.random.normal(ks[2], (E, D, 2 * F), jnp.float32) * scale, 'w_down': jax.random.normal(ks[3], (E, F, D), jnp.float32) * scale, 'shared_gate_up': jax.random.normal(ks[4], (D, 2 * F), jnp.float32) * scale, 'shared_down': jax.random.normal(ks[5], (F, D), jnp.float32) * scale}
    _L0_ffn_in = _L0_ffn_setup()
    _L0_c = _w((lambda *s: np.random.randn(*s).astype(np.float32) * 0.05)(8, 256))
    _L0_wmod = _w((lambda *s: np.random.randn(*s).astype(np.float32) * 0.05)(256, 6 * 256) * 256 ** (-0.5))
    _d = {'L0_attn_u': _L0_attn_in['u'], 'L0_attn_in_proj_w': _L0_attn_in['in_proj_w'], 'L0_attn_in_proj_b': _L0_attn_in['in_proj_b'], 'L0_attn_conv_w': _L0_attn_in['conv_w'], 'L0_attn_conv_b': _L0_attn_in['conv_b'], 'L0_attn_dt_bias': _L0_attn_in['dt_bias'], 'L0_attn_A_log': _L0_attn_in['A_log'], 'L0_attn_ln_w': _L0_attn_in['ln_w'], 'L0_attn_ln_b': _L0_attn_in['ln_b'], 'L0_attn_out_proj_w': _L0_attn_in['out_proj_w'], 'L0_attn_out_proj_b': _L0_attn_in['out_proj_b'], 'L0_ffn_router_w': _L0_ffn_in['router_w'], 'L0_ffn_w_gate_up': _L0_ffn_in['w_gate_up'], 'L0_ffn_w_down': _L0_ffn_in['w_down'], 'L0_ffn_shared_gate_up': _L0_ffn_in['shared_gate_up'], 'L0_ffn_shared_down': _L0_ffn_in['shared_down'], 'L0_c': _L0_c, 'L0_wmod': _L0_wmod}
    _x0 = _d['L0_attn_u']
    _d['L0_attn_u'] = jax.random.normal(jax.random.fold_in(jax.random.key(seed), 1), (8, 512, 256), dtype=_x0.dtype)
    del _x0
    return _d

def reference(L0_attn_u, L0_attn_in_proj_w, L0_attn_in_proj_b, L0_attn_conv_w, L0_attn_conv_b, L0_attn_dt_bias, L0_attn_A_log, L0_attn_ln_w, L0_attn_ln_b, L0_attn_out_proj_w, L0_attn_out_proj_b, L0_ffn_router_w, L0_ffn_w_gate_up, L0_ffn_w_down, L0_ffn_shared_gate_up, L0_ffn_shared_down, L0_c, L0_wmod):

    def _L0_attn_ref(u, in_proj_w, in_proj_b, conv_w, conv_b, dt_bias, A_log, ln_w, ln_b, out_proj_w, out_proj_b):
        import jax, jax.numpy as jnp
        import numpy as np
        D_MODEL = 256
        D_STATE = 64
        D_CONV = 4
        EXPAND = 2
        HEADDIM = 128
        NGROUPS = 1
        CHUNK = 32
        D_INNER = EXPAND * D_MODEL
        NHEADS = D_INNER // HEADDIM
        CONV_DIM = D_INNER + 2 * NGROUPS * D_STATE
        D_IN_PROJ = 2 * D_INNER + 2 * NGROUPS * D_STATE + NHEADS
        BATCH = 2
        SEQLEN = 512
        LN_EPS = 1e-05

        def segsum(x):
            T = x.shape[-1]
            xe = jnp.broadcast_to(x[..., None], (*x.shape, T))
            strict_lower = jnp.tril(jnp.ones((T, T), bool), -1)
            xe = jnp.where(strict_lower, xe, 0.0)
            s = jnp.cumsum(xe, axis=-2)
            lower = jnp.tril(jnp.ones((T, T), bool), 0)
            return jnp.where(lower, s, -jnp.inf)

        def ssd_minimal_discrete(X, A, B, C, block_len):
            b, length = (X.shape[0], X.shape[1])
            pad = -length % block_len
            if pad:
                padt = lambda t: jnp.pad(t, [(0, 0), (0, pad)] + [(0, 0)] * (t.ndim - 2))
                X, A, B, C = (padt(X), padt(A), padt(B), padt(C))
            c = (length + pad) // block_len
            X = X.reshape(b, c, block_len, NHEADS, HEADDIM)
            B = B.reshape(b, c, block_len, NHEADS, D_STATE)
            C = C.reshape(b, c, block_len, NHEADS, D_STATE)
            A = A.reshape(b, c, block_len, NHEADS).transpose(0, 3, 1, 2)
            A_cumsum = jnp.cumsum(A, axis=-1)
            L = jnp.exp(segsum(A))
            Y_diag = jnp.einsum('bclhn,bcshn,bhcls,bcshp->bclhp', C, B, L, X)
            decay_states = jnp.exp(A_cumsum[:, :, :, -1:] - A_cumsum)
            states = jnp.einsum('bclhn,bhcl,bclhp->bchpn', B, decay_states, X)
            init = jnp.zeros_like(states[:, :1])
            states = jnp.concatenate([init, states], axis=1)
            A_last = jnp.pad(A_cumsum[:, :, :, -1], ((0, 0), (0, 0), (1, 0)))
            decay_chunk = jnp.exp(segsum(A_last))
            new_states = jnp.einsum('bhzc,bchpn->bzhpn', decay_chunk, states)
            states = new_states[:, :-1]
            state_decay_out = jnp.exp(A_cumsum)
            Y_off = jnp.einsum('bclhn,bchpn,bhcl->bclhp', C, states, state_decay_out)
            Y = (Y_diag + Y_off).reshape(b, c * block_len, NHEADS, HEADDIM)
            return Y[:, :length]
        b, seqlen, _ = u.shape
        zxbcdt = jnp.einsum('bld,ed->ble', u, in_proj_w) + in_proj_b
        z = zxbcdt[..., :D_INNER]
        xBC = zxbcdt[..., D_INNER:D_INNER + CONV_DIM]
        dt = zxbcdt[..., D_INNER + CONV_DIM:]
        dt = jax.nn.softplus(dt + dt_bias)
        A = -jnp.exp(A_log)
        xc = jnp.transpose(xBC, (0, 2, 1))
        xc = jnp.pad(xc, ((0, 0), (0, 0), (D_CONV - 1, 0)))
        xc = jax.lax.conv_general_dilated(xc, conv_w, (1,), 'VALID', feature_group_count=CONV_DIM, dimension_numbers=('NCH', 'OIH', 'NCH'))
        xc = xc + conv_b[None, :, None]
        xBC = jax.nn.silu(jnp.transpose(xc, (0, 2, 1)))
        x = xBC[..., :D_INNER].reshape(b, seqlen, NHEADS, HEADDIM)
        Bm = xBC[..., D_INNER:D_INNER + NGROUPS * D_STATE]
        Cm = xBC[..., D_INNER + NGROUPS * D_STATE:]
        Bh = jnp.broadcast_to(Bm[:, :, None, :], (b, seqlen, NHEADS, D_STATE))
        Ch = jnp.broadcast_to(Cm[:, :, None, :], (b, seqlen, NHEADS, D_STATE))
        y = ssd_minimal_discrete(x * dt[..., None], A * dt, Bh, Ch, CHUNK)
        y = y.reshape(b, seqlen, D_INNER)
        y = y * jax.nn.silu(z)
        mu = jnp.mean(y, axis=-1, keepdims=True)
        var = jnp.mean(jnp.square(y - mu), axis=-1, keepdims=True)
        y = (y - mu) * jax.lax.rsqrt(var + LN_EPS) * ln_w + ln_b
        return jnp.einsum('ble,de->bld', y, out_proj_w) + out_proj_b

    def _L0_ffn_ref(hidden_states, router_w, w_gate_up, w_down, shared_gate_up, shared_down):
        import jax, jax.numpy as jnp
        import numpy as np
        B, S, D, F, E, K = (2, 256, 256, 512, 8, 1)

        def _silu_mul(gu):
            g, u = jnp.split(gu, 2, axis=-1)
            return jax.nn.silu(g) * u

        def _moe_forward(hidden_states, router_w, w_gate_up, w_down, shared_gate_up, shared_down, top_k=K):
            b, s, d = hidden_states.shape
            x = hidden_states.reshape(-1, d)
            router_logits = x @ router_w.T
            topk_vals, topk_ids = jax.lax.top_k(router_logits, top_k)
            gate = jax.nn.sigmoid(topk_vals.astype(jnp.float32)).astype(x.dtype)
            xs = (x[:, None, :] * gate[:, :, None]).reshape(-1, d)
            ids_flat = topk_ids.reshape(-1)
            n_experts = w_gate_up.shape[0]

            def body(acc, inp):
                wg, wd, e = inp
                h = _silu_mul(xs @ wg)
                o = h @ wd
                mask = (ids_flat == e)[:, None]
                return (acc + jnp.where(mask, o, jnp.zeros((), o.dtype)), None)
            acc0 = jnp.zeros_like(xs)
            routed, _ = jax.lax.scan(body, acc0, (w_gate_up, w_down, jnp.arange(n_experts)))
            routed = routed.reshape(-1, top_k, d).sum(1)
            shared = _silu_mul(x @ shared_gate_up) @ shared_down
            return (routed + shared).reshape(b, s, d)
        return _moe_forward(hidden_states, router_w, w_gate_up, w_down, shared_gate_up, shared_down)
    x = L0_attn_u
    mod = (_silu(L0_c) @ L0_wmod).reshape(L0_c.shape[0], 6, 1, -1)
    sa, ca, ga, sb, cb, gb = (mod[:, 0], mod[:, 1], mod[:, 2], mod[:, 3], mod[:, 4], mod[:, 5])
    ga = (2 * (ga >= 0) - 1) * jnp.maximum(jnp.abs(ga), 0.25)
    gb = (2 * (gb >= 0) - 1) * jnp.maximum(jnp.abs(gb), 0.25)
    h = _layernorm(x, axis=-1) * (1 + ca) + sa
    x = x + ga * _L0_attn_ref(h, L0_attn_in_proj_w, L0_attn_in_proj_b, L0_attn_conv_w, L0_attn_conv_b, L0_attn_dt_bias, L0_attn_A_log, L0_attn_ln_w, L0_attn_ln_b, L0_attn_out_proj_w, L0_attn_out_proj_b)
    h = _layernorm(x, axis=-1) * (1 + cb) + sb
    x = x + gb * _L0_ffn_ref(h, L0_ffn_router_w, L0_ffn_w_gate_up, L0_ffn_w_down, L0_ffn_shared_gate_up, L0_ffn_shared_down)
    return x

_drawn_inputs = setup_inputs


def setup_inputs(seed=0):
    import zlib

    import numpy as np

    out = dict(_drawn_inputs(seed))
    spreads = {'L0_attn_ln_w': (1.0, 0.2), 'L0_attn_ln_b': (0.0, 0.351)}
    factors = {'L0_attn_in_proj_b': 8.0,
     'L0_attn_conv_b': 8.0,
     'L0_attn_out_proj_b': 8.0,
     'L0_ffn_router_w': 8.0,
     'L0_ffn_w_gate_up': 8.0,
     'L0_ffn_w_down': 8.0,
     'L0_ffn_shared_gate_up': 8.0,
     'L0_ffn_shared_down': 8.0}
    for name, (base, spread) in spreads.items():
        noise = np.random.default_rng([zlib.crc32(name.encode()), seed]).standard_normal(out[name].shape)
        drawn = base * np.exp(spread * noise) if base else spread * noise
        out[name] = jnp.asarray(drawn.astype(out[name].dtype))
    for name, factor in factors.items():
        out[name] = (out[name] * factor).astype(out[name].dtype)
    return out
```

```python
from contextlib import ExitStack

import concourse.bass as bass
from concourse import mybir

F32 = mybir.dt.float32
I32 = mybir.dt.int32
ALU = mybir.AluOpType
ACT = mybir.ActivationFunctionType
AX = mybir.AxisListType

P = 128
NB, SEQ, D = 8, 512, 256
NC = SEQ // P
H, HD, NS = 4, 128, 64
DI = H * HD
NT = 5
NPROJ = 2 * DI + 2 * NS + H
E, F = 8, 512
KD, KF, KI = D // P, F // P, DI // P
WE = KD * 2 * F + KF * D
TOK = NB * SEQ
REG = TOK + P
NBLK = TOK // P + E - 1
ROW = 3 * D + 1
LATE = 7
EPS = 1e-5
LOG_TERMS = 9

CW, CB, IB, LW, LB = 0, 20, 25, 30, 34
NCOL = 38
ZB, DTB, DTB2, AL, OB = 0, 512, 516, 520, 524
NROW = 780
C_ID, C_LE, C_GT, C_LT, C_ONE = (k * P for k in range(5))
C_TIE = 5 * P
C_REG = C_TIE + E
C_TID = C_REG + E
C_P = C_TID + NC
C_CMP = C_P + 1
C_I = C_CMP + TOK // P
C_OFF = C_I + NBLK * E
C_E = C_OFF + NBLK * E
NCONST = C_E + E

T_ORDER = ["cu0", "cu1", "AhT0", "AhT1", "cu2", "yT0", "cu3", "yT1", "AtB", "h2T0", "AtX0", "yT2", "AtX1", "h2T1",
           "AtX2", "yT3", "AtX3", "h2T2", "h2T3", "dn0", "dn1", "dn2", "dn3"]
W_ORDER = ["AxB", "Ax0", "Ax1", "Ax2", "Ax3", "Az0", "Az1", "Az2", "Az3", "Cg0", "Cu0", "Cg2", "Cu2"]


class Batch:

    def __init__(self, i, par):
        self.i, self.par = i, par

    def next(self):
        return Batch(self.i, 1) if self.par == 0 else Batch(self.i + 1, 0)

    def plus(self, k):
        return self if k == 0 else self.next().plus(k - 1)

    def num(self, add=0):
        return self.i * 2 + (self.par + add)


class Count:

    def __init__(self, sem, per, step=1):
        self.sem, self.per, self.step = sem, per, step

    def at(self, b, k):
        return b.i * (2 * self.per * self.step) + (self.per * b.par + k + 2 * self.per) * self.step

    def start(self, eng, batches=2):
        eng.sem_inc(self.sem, batches * self.per * self.step)


class Slot:

    def __init__(self, ap, full, free, uses):
        self.ap, self.uses = ap, uses
        self.full, self.free = Count(full, len(uses)), Count(free, len(uses))

    def index(self, use, mode):
        if mode == "pro":
            return [u for u in self.uses if u[0] == "A"].index(use)
        if mode == "last":
            return [u for u in self.uses if u[0] != "A"].index(use)
        return self.uses.index(use)


class Turn:

    def __init__(self, b, mode):
        self.b, self.mode = b, mode
        self.n = None if mode == "last" else b.next()


class Chain:

    def __init__(self, eng, count):
        self.eng, self.count, self.k, self.b = eng, count, 0, None

    def begin(self, b):
        self.b, self.k = b, 0

    def link(self, ins, apart=None):
        self.k += 1
        ins.then_inc(self.count.sem, 1)
        self.eng.wait_ge(self.count.sem, self.count.at(self.b, self.k))
        if apart:
            apart(self.eng)

    def end(self):
        assert self.k == self.count.per, ("steps of this chain in a batch", self.k)


def build(nc, u, w_in, w_out, w_router, w_mod, c_t, w_experts, w_shared, cols_in, rows_in, consts_in, out):
    ctx = ExitStack()
    with ctx:
        def sb(name, shape, dt=F32):
            return ctx.enter_context(nc.sbuf_tensor(name, shape, dt))

        def sem(name):
            return ctx.enter_context(nc.semaphore(name))

        slots = nc.dram_tensor("slots", (E * REG + P, ROW), F32, kind="Internal").ap()
        mod_dram = nc.dram_tensor("mod_rows", (NB, 4 * D), F32, kind="Internal").ap()

        We = sb("We", [P, E * WE])
        top = We[:, (E - LATE) * WE:]
        used = [0]

        def early(n):
            used[0] += n
            assert used[0] <= LATE * WE
            return top[:, used[0] - n:used[0]]

        Ws = sb("Ws", [P, WE])
        Wsg = Ws[:, 0:KD * 2 * F].rearrange("p (k n) -> p k n", k=KD)
        Wsd = Ws[:, KD * 2 * F:].rearrange("p (k n) -> p k n", k=KF)
        Xt = [early(NC * DI).rearrange("p (c n) -> p c n", c=NC) for _ in range(2)]
        Zs = [early(NC * DI).rearrange("p (c n) -> p c n", c=NC) for _ in range(2)]
        Win = early(KD * NPROJ).rearrange("p (k n) -> p k n", k=KD)
        xpre = [early(3 + SEQ) for _ in range(2)]
        Wout = sb("Wout", [P, KI, D])
        Wr = sb("Wr", [P, KD, E])
        Wmod = We[:, 0:KD * 6 * D].rearrange("p (k n) -> p k n", k=KD)
        colp = sb("colp", [P, NCOL])
        rowp = sb("rowp", [P, NROW])
        K = sb("K", [P, NCONST])
        ident, LE, GT, LT, ONE = (K[:, c:c + P] for c in (C_ID, C_LE, C_GT, C_LT, C_ONE))
        cT = sb("cT", [P, KD, NB])
        cTs = sb("cTs", [P, KD, NB])
        cth = sb("cth", [P, KD, NB])
        modc = sb("modc", [P, 4, NB])
        modb = sb("modb", [P, 4])
        brow = sb("brow", [P, D])
        negA = sb("negA", [P, H])
        dtb = sb("dtb", [P, H])

        xin = [sb(f"xin{q}", [P, NC, D]) for q in range(2)]
        mrow = [sb(f"mrow{q}", [P, 4, D]) for q in range(2)]
        gab = sb("gab", [P, D])
        hn = sb("hn", [P, NC, D])
        hT = sb("hT", [P, KD, SEQ])
        acc = [sb(f"acc{q}", [P, SEQ]) for q in range(2)]
        th = [sb(f"th{q}", [P, SEQ]) for q in range(2)]
        xs = [early(SEQ) for _ in range(2)]
        BCs = [early(SEQ) for _ in range(2)]
        CT = [early(SEQ) for _ in range(2)]
        Btok = [sb(f"Btok{q}", [P, NC, NS]) for q in range(2)]
        zh = [early(DI) for _ in range(2)]
        zth = [early(DI) for _ in range(2)]
        dts = sb("dts", [P, 8, NC * H])
        dt = [sb(f"dt{q}", [P, NC, H]) for q in range(2)]
        da = [sb(f"da{q}", [P, NC, H]) for q in range(2)]
        arhs = [early(H * P).rearrange("p (h l) -> p h l", h=H) for _ in range(NC)]
        Ex = [early(H * P).rearrange("p (h l) -> p h l", h=H) for _ in range(2)]
        ec = [sb(f"ec{c}", [P, 3 * H]) for c in range(NC)]
        Gm = early(P)
        Wm = early(H * P).rearrange("p (h l) -> p h l", h=H)
        Bh = early(H * NS).rearrange("p (h n) -> p h n", h=H)
        St = sb("St", [NS, H, HD])
        y = [sb(f"y{q}", [P, DI]) for q in range(2)]
        yn = [sb(f"yn{q}", [P, DI]) for q in range(2)]
        yT = sb("yT", [P, KI, P])
        t1 = sb("t1", [P, D])
        st = sb("st", [P, 6])
        mvy = [sb(f"mvy{q}", [P, 3]) for q in range(2)]
        mvx = [sb(f"mvx{q}", [P, 3]) for q in range(2)]
        power = sb("power", [P, NC])
        vl1 = sb("vl1", [P, NC])
        rs = [sb(f"ry{q}", [P, 2]) for q in range(2)]
        rs2 = [sb(f"rx{q}", [P, 2]) for q in range(2)]
        st1 = sb("st1", [P, NC, 6])
        mv1 = sb("mv1", [P, NC, 2])
        rs1 = sb("rs1", [P, NC])
        n2 = [sb(f"n2{q}", [P, D]) for q in range(2)]
        h2 = sb("h2", [P, NC, D])
        h2T = sb("h2T", [P, KD, SEQ])
        rowbuf = sb("rowbuf", [P, NC, ROW])
        hid = sb("hid", [P, KF, SEQ])
        lg = sb("lg", [P, NC, E])
        rt = sb("rt", [P, 4, NC, E])
        mx = sb("mx", [P, 4, NC])
        onehot = sb("onehot", [P, NC, E])
        carry = sb("carry", [P, NC + 1, E])
        posf = sb("posf", [P, NC])
        posi = sb("posi", [P, NC], I32)
        tidf = sb("tidf", [P, NC])
        padf = sb("padf", [P, E])
        padi = sb("padi", [P, E], I32)
        tab = sb("tab", [P, 6, E])
        tabr = sb("tabr", [P, 2, NBLK])
        tabi = sb("tabi", [P, 2, NBLK], I32)

        mpre = h2T[0:NB, :, :].rearrange("b k n -> b (k n)")
        mabs, msgn = hid[0:NB, 0, :], hid[0:NB, 1, :]
        lnb_b = hid[:, 2, :].rearrange("p (k n) -> p k n", k=KI)
        padrow = xin[0][:, :, :].rearrange("p c d -> p (c d)")[:, 0:ROW]
        tabj = hid[:, 0, 0:E * (TOK // P)].rearrange("p (e j) -> p e j", e=E)
        tabb = xin[1][:, :, :].rearrange("p c d -> p (c d)")[:, 0:3 * NBLK * E].rearrange("p (m i e) -> p m i e", m=3, e=E)

        bx = [hn[:, q, :] for q in range(2)]
        brest = [rowbuf[:, 2 * q, 0:2 * D + 1] for q in range(2)]
        bxT = [h2T[:, :, q * P:(q + 1) * P] for q in range(2)]
        bth = [th[q][:, :] for q in range(2)]
        bhg = [acc[q][:, :] for q in range(2)]
        bhid = [y[q][:, :] for q in range(2)]
        bhT = [yn[q][:, :].rearrange("p (k n) -> p k n", k=KF) for q in range(2)]
        bt = [n2[q][:, :] for q in range(2)]
        bo = [h2[:, q, :] for q in range(2)]

        def pb(name):
            return ctx.enter_context(nc.psum_tensor(name, [P, 512], F32))

        banks = {n: pb("ps" + n) for n in ("T0", "T1", "W0", "W1", "SG", "YD", "YO", "M")}

        def slot(name, ap, uses):
            return Slot(ap, sem(f"{name}_full"), sem(f"{name}_free"), uses)

        T = [slot(f"T{q}", banks[f"T{q}"][:, :], T_ORDER[q::2]) for q in range(2)]
        W = [slot(f"W{q}", banks[f"W{q}"][:, :], W_ORDER[q::2]) for q in range(2)]
        SG = slot("SG", banks["SG"][:, :], ["seg0"] + [f"{w}{c + k}" for c in range(NC - 1) for k, w in ((1, "seg"), (0, "dS"))])
        YD = slot("YD", banks["YD"][:, :], [f"yd{c}" for c in range(NC)] + ["Cg1", "Cg3"])
        YO = slot("YO", banks["YO"][:, :], ["g0", "g1"] + [f"{w}{c + k}" for c in range(1, NC - 1) for k, w in ((1, "g"), (0, "yo"))] + [f"yo{NC - 1}", "Cu1", "Cu3"])
        M = banks["M"]
        MM = slot("M", M[:, :], ["Adt", "op0", "op1", "op2", "op3", "rt", "rk"])
        SLOTS = [*T, *W, SG, YD, YO, MM]
        WHERE = {use: s for s in SLOTS for use in s.uses}

        def count(name, per, step=1):
            return Count(sem(name), per, step)

        x_loaded = [sem("x_loaded0"), sem("x_loaded1")]
        mod_loaded = [sem("mod_loaded0"), sem("mod_loaded1")]
        ct_moved = count("ct_moved", 1, 16)
        scattered = sem("scattered")
        hT_ready = count("hT_ready", KD)
        xpre_ready = count("xpre_ready", NT)
        tap_ready = count("tap_ready", NT)
        th_ready = count("th_ready", NT)
        zth_ready = count("zth_ready", NC)
        dte_ready = count("dte_ready", 1)
        btok_ready = count("btok_ready", 1)
        E_ready = count("E_ready", NC)
        ec_ready = count("ec_ready", NC)
        yn_ready = count("yn_ready", NC)
        yT_ready = count("yT_ready", NC)
        n2_ready = count("n2_ready", NC)
        h2T_ready = count("h2T_ready", NC)
        gth_ready = count("gth_ready", 1)
        gbrow_ready = count("gbrow_ready", 1)
        fth_ready = count("fth_ready", KF)
        dve_a = count("dve_a", 6 + LOG_TERMS + 2 * NT)
        dve_b = count("dve_b", 6 * NC + 8)
        dve_l = count("dve_l", 2)
        dtx_ready = count("dtx_ready", 1)
        dt_ready = count("dt_ready", 1)
        conv_ready = count("conv_ready", NT)
        xs_ready = count("xs_ready", NT)
        X_ready = count("X_ready", H)
        zh_ready = count("zh_ready", NC)
        W_ready = count("W_ready", NC)
        S_ready = count("S_ready", NC - 1)
        y_var = count("y_var", NC)
        x1_var = count("x1_var", NC)
        x1_ready = count("x1_ready", NC)
        modb_ready = count("modb_ready", 1)
        gab_ready = count("gab_ready", 1)
        ln1_stats = count("ln1_stats", 1)
        onehot_ready = count("onehot_ready", 1)
        gate_ready = count("gate_ready", 1)
        pos_ready = count("pos_ready", 1)
        hid_ready = count("hid_ready", KF)
        base_ready = count("base_ready", NC)
        z_ready = count("z_ready", NC)
        y_power = count("y_power", NC)
        y_stats = count("y_stats", NC)
        x1_power = count("x1_power", NC)
        x1_stats = count("x1_stats", NC)
        ln1_power = count("ln1_power", 1)
        hn_ready = count("hn_ready", NC)
        arhs_ready = count("arhs_ready", NC)
        Bh_ready = count("Bh_ready", NC - 1)
        xg_ready = count("xg_ready", 1)
        h2_scaled = count("h2_scaled", NC)
        h2_ready = count("h2_ready", NC)
        h2g_ready = count("h2g_ready", NC)
        BY_ACT = [hT_ready, xpre_ready, tap_ready, th_ready, zth_ready, dte_ready, btok_ready, E_ready,
                  ec_ready, yn_ready, yT_ready, n2_ready, h2T_ready, gth_ready, gbrow_ready, fth_ready]
        BY_DVE = [dve_a, dve_b, dve_l, dtx_ready, dt_ready, conv_ready, xs_ready, X_ready, zh_ready, W_ready,
                  S_ready, y_var, x1_ready, x1_var, modb_ready, gab_ready, ln1_stats, onehot_ready,
                  gate_ready, pos_ready, hid_ready, base_ready, z_ready]
        BY_POOL = [y_power, y_stats, x1_power, x1_stats, ln1_power, hn_ready, arhs_ready, Bh_ready, xg_ready, h2_scaled, h2_ready, h2g_ready]

        consts_in_sb = sem("consts_in_sb")
        win_in, wout_in, ws_in = sem("win_in"), sem("wout_in"), sem("ws_in")
        we_low, we_high = sem("we_low"), sem("we_high")
        cth_done, cs_done, modmm_done, mod_set, mod_stored = (sem(n) for n in (
            "cth_done", "cs_done", "modmm_done", "mod_set", "mod_stored"))
        lnb_done, bmm_done, setup_dve, neg_done, setup_pool, setup_ready = (sem(n) for n in (
            "lnb_done", "bmm_done", "setup_dve", "neg_done", "setup_pool", "setup_ready"))
        pad_ready, pad_stored, tab_ready, tab_dve = (sem(n) for n in (
            "pad_ready", "pad_stored", "tab_ready", "tab_dve"))
        scan_over, power_set, passed = sem("scan_over"), sem("power_set"), sem("passed")

        FIRST = Batch(0, 0)
        BEFORE = Batch(-1, 1)

        def opened(pe, t, use):
            s = WHERE[use]
            pe.wait_ge(s.free.sem, s.free.at(t.b, s.index(use, t.mode)))
            return s.ap

        def filled(eng, t, use):
            s = WHERE[use]
            eng.wait_ge(s.full.sem, s.full.at(t.b, s.index(use, t.mode) + 1))
            return s.ap

        def rows_left(eng, b):
            eng.wait_ge(scattered, b.i * (2 * 16 * NC) + 16 * (NC * b.par + 1))

        def emptied(eng, t, use):
            s = WHERE[use]
            eng.wait_ge(s.free.sem, s.free.at(t.b, s.index(use, t.mode) + 1))

        def fill(use, ins):
            ins.then_inc(WHERE[use].full.sem, 1)

        def empty(use, ins):
            ins.then_inc(WHERE[use].free.sem, 1)

        def wait(eng, count, b, k):
            eng.wait_ge(count.sem, count.at(b, k))

        def apart(eng):
            eng.sem_inc(passed, 1)

        def turns(eng, body):
            with eng.Fori(0, NB // 2 - 1) as i:
                body(Turn(Batch(i, 0), "full"), True)
                body(Turn(Batch(i, 1), "full"), True)
            body(Turn(Batch(NB // 2 - 1, 0), "full"), False)
            body(Turn(Batch(NB // 2 - 1, 1), "last"), False)


        bx_loaded = [sem("bx_loaded0"), sem("bx_loaded1")]
        rest_loaded = [sem("rest_loaded0"), sem("rest_loaded1")]
        row_out = [sem("row_out0"), sem("row_out1")]
        bturned, gfull, ufull, hturned, dfull = (count(n, 1) for n in (
            "bturned", "gfull", "ufull", "hturned", "dfull"))
        bxT_ready, bth_ready, bhT_ready = (count(n, 1) for n in ("bxT_ready", "bth_ready", "bhT_ready"))
        bhg_ready, bhid_ready, bt_ready, bo_ready = (count(n, 1) for n in (
            "bhg_ready", "bhid_ready", "bt_ready", "bo_ready"))
        Gb, Ub = [banks["W0"], banks["YD"]], [banks["W1"], banks["YO"]]

        def blocks(eng, body):
            pairs = (NBLK - 2) // 2
            with eng.Fori(0, pairs) as i:
                body(Batch(i, 0), 2)
                body(Batch(i, 1), 2)
            for j in range(2 * pairs, NBLK):
                body(Batch(j // 2, j % 2), min(2, NBLK - 1 - j))

        def table(eng, row, b, most):
            j = b.num()
            return eng.value_load(tabi[0:1, row, bass.ds(j, 1)], min_val=0, max_val=most)

        def landed(eng, sems, b):
            eng.wait_ge(sems[b.par], b.i * 16 + 16)

        def slots_complete(eng):
            eng.wait_ge(tab_ready, 1)
            rows_left(eng, Batch(NB // 2, 0))
            eng.wait_ge(pad_stored, 16 * E)

        def routed_sync(sp):
            slots_complete(sp)

            def load(b):
                first = table(sp, 0, b, E * REG)
                sp.dma_start(bx[b.par], slots[bass.ds(first, P), 0:D]).then_inc(bx_loaded[b.par], 16)

            load(Batch(0, 0))
            load(Batch(0, 1))

            def body(b, ahead):
                if ahead == 2:
                    wait(sp, bturned, b, 1)
                    apart(sp)
                    load(b.plus(2))

            blocks(sp, body)

        def routed_tensor(pe):
            for cnt in (bturned, gfull, ufull, hturned, dfull):
                cnt.start(pe)
            pe.wait_ge(tab_ready, 1)

            def turn_block(b):
                landed(pe, bx_loaded, b)
                wait(pe, bxT_ready, b, -1)
                for k in range(KD):
                    ins = pe.transpose(banks[f"T{b.par}"][:, k * P:(k + 1) * P], bx[b.par][:, k * P:(k + 1) * P], ident)
                ins.then_inc(bturned.sem, 1)

            def gate_up(b):
                at = table(pe, 1, b, (E - 1) * WE)
                wait(pe, bxT_ready, b, 1)
                for ps, done, used_up, first in ((Gb[b.par], gfull, bhg_ready, 0), (Ub[b.par], ufull, bhid_ready, F)):
                    wait(pe, used_up, b, -1)
                    for k in range(KD):
                        ins = pe.matmul(ps[:, :], bxT[b.par][:, k, :], We[:, bass.ds(at + (2 * F * k + first), F)],
                                        start=(k == 0), stop=(k == KD - 1))
                    ins.then_inc(done.sem, 1)

            def turn_hidden(b):
                wait(pe, bhid_ready, b, 1)
                wait(pe, bhT_ready, b, 0)
                for k in range(KF):
                    ins = pe.transpose(banks["SG"][:, k * P:(k + 1) * P], bhid[b.par][:, k * P:(k + 1) * P], ident)
                ins.then_inc(hturned.sem, 1)

            def down(b):
                at = table(pe, 1, b, (E - 1) * WE)
                wait(pe, bhT_ready, b, 1)
                wait(pe, bt_ready, b, 0)
                for k in range(KF):
                    ins = pe.matmul(M[:, 0:D], bhT[b.par][:, k, :],
                                    We[:, bass.ds(at + (KD * 2 * F + D * k), D)], start=(k == 0), stop=(k == KF - 1))
                ins.then_inc(dfull.sem, 1)

            turn_block(Batch(0, 0))
            pe.wait_ge(we_low, 16)
            pe.wait_ge(we_high, 16)
            gate_up(Batch(0, 0))
            turn_block(Batch(0, 1))

            def body(b, ahead):
                turn_hidden(b)
                if ahead >= 1:
                    gate_up(b.plus(1))
                if ahead == 2:
                    turn_block(b.plus(2))
                down(b)

            blocks(pe, body)

        def routed_scalar(act):
            for cnt in (bxT_ready, bth_ready, bhT_ready):
                cnt.start(act)

            def evac_block(b):
                wait(act, bturned, b, 1)
                act.activation(bxT[b.par], banks[f"T{b.par}"][:, 0:KD * P].rearrange("p (k n) -> p k n", k=KD), ACT.Copy)\
                    .then_inc(bxT_ready.sem, 1)

            def tanh_gate(b):
                wait(act, gfull, b, 1)
                wait(act, bhg_ready, b, -1)
                act.activation(bth[b.par], Gb[b.par][:, :], ACT.Tanh, scale=0.5).then_inc(bth_ready.sem, 1)

            def evac_hidden(b):
                wait(act, hturned, b, 1)
                act.activation(bhT[b.par], banks["SG"][:, :].rearrange("p (k n) -> p k n", k=KF), ACT.Copy).then_inc(bhT_ready.sem, 1)

            evac_block(Batch(0, 0))
            tanh_gate(Batch(0, 0))
            evac_block(Batch(0, 1))

            def body(b, ahead):
                evac_hidden(b)
                if ahead >= 1:
                    tanh_gate(b.plus(1))
                if ahead == 2:
                    evac_block(b.plus(2))

            blocks(act, body)

        def routed_vector(dve):
            for cnt in (bhg_ready, bhid_ready, bt_ready, bo_ready):
                cnt.start(dve)
            steps = [0]

            def link(ins):
                steps[0] += 1
                ins.then_inc(tab_dve, 1)
                dve.wait_ge(tab_dve, steps[0])

            link(dve.tensor_scalar(padf[:, :], carry[:, 0, :], K[:, C_P:C_P + 1], None, ALU.add))
            dve.tensor_copy(padi[:, :], padf[:, :]).then_inc(pad_ready, 1)
            link(dve.tensor_tensor(tab[:, 0, :], carry[:, 0, :], K[:, C_REG:C_REG + E], ALU.subtract))
            link(dve.tensor_tensor(tabj[:, :, :], tab[:, 0, :].unsqueeze(2).broadcast_to([P, E, TOK // P]),
                                   K[:, C_CMP:C_CMP + TOK // P].unsqueeze(1).broadcast_to([P, E, TOK // P]), ALU.is_gt))
            link(dve.tensor_reduce(tab[:, 1, :], tabj[:, :, :], AX.X, ALU.add))
            link(dve.tensor_copy(tab[:, 2, :], tab[:, 1, :]))
            for e in range(1, E):
                link(dve.tensor_tensor(tab[:, 2, e:e + 1], tab[:, 2, e - 1:e], tab[:, 1, e:e + 1], ALU.add))
            link(dve.tensor_tensor(tab[:, 3, :], tab[:, 2, :], tab[:, 1, :], ALU.subtract))
            link(dve.tensor_scalar(tab[:, 4, :], tab[:, 3, :], float(-P), None, ALU.mult))
            wide = lambda a: a.unsqueeze(1).broadcast_to([P, NBLK, E])
            ci = K[:, C_I:C_I + NBLK * E].rearrange("p (i e) -> p i e", e=E)
            co = K[:, C_OFF:C_OFF + NBLK * E].rearrange("p (i e) -> p i e", e=E)
            link(dve.tensor_tensor(tabb[:, 0], ci, wide(tab[:, 2, :]), ALU.is_ge))
            link(dve.tensor_tensor(tabb[:, 1], ci, wide(tab[:, 3, :]), ALU.is_ge))
            link(dve.tensor_tensor(tabb[:, 2], tabb[:, 1], tabb[:, 0], ALU.subtract))
            link(dve.tensor_tensor(tabb[:, 0], co, wide(tab[:, 4, :]), ALU.add))
            link(dve.tensor_tensor(tabb[:, 0], tabb[:, 0], tabb[:, 2], ALU.mult))
            link(dve.tensor_reduce(tabr[:, 0, :], tabb[:, 0], AX.X, ALU.add))
            link(dve.tensor_scalar(tabr[:, 0, :], tabr[:, 0, :], float(E * REG), None, ALU.add))
            link(dve.tensor_tensor(tabb[:, 1], tabb[:, 2], wide(K[:, C_E:C_E + E]), ALU.mult))
            link(dve.tensor_reduce(tabr[:, 1, :], tabb[:, 1], AX.X, ALU.add))
            dve.tensor_copy(tabi[:, :, :], tabr[:, :, :]).then_inc(tab_ready, 1)

            def hidden(b):
                q = b.par
                wait(dve, bth_ready, b, 1)
                dve.scalar_tensor_tensor(out=bhg[q], in0=bth[q], scalar=1.0, in1=Gb[q][:, :], op0=ALU.add, op1=ALU.mult)\
                    .then_inc(bhg_ready.sem, 1)
                wait(dve, ufull, b, 1)
                wait(dve, bhg_ready, b, 1)
                dve.tensor_tensor(bhid[q], bhg[q], Ub[q][:, :], ALU.mult).then_inc(bhid_ready.sem, 1)

            def combine(b):
                q = b.par
                wait(dve, dfull, b, 1)
                landed(dve, rest_loaded, b)
                dve.scalar_tensor_tensor(out=bt[q], in0=M[:, 0:D], scalar=0.5, in1=brest[q][:, D:2 * D],
                                         op0=ALU.mult, op1=ALU.mult).then_inc(bt_ready.sem, 1)
                wait(dve, bt_ready, b, 1)
                dve.tensor_tensor(bo[q], bt[q], brest[q][:, 0:D], ALU.add).then_inc(bo_ready.sem, 1)

            hidden(Batch(0, 0))

            def body(b, ahead):
                if ahead >= 1:
                    hidden(b.plus(1))
                combine(b)

            blocks(dve, body)

        def routed_gpsimd(pool):
            pool.memset(padrow[:, :], 0.0).then_inc(setup_pool, 1)
            pool.wait_ge(setup_pool, 3)
            pool.memset(padrow[:, 3 * D:].bitcast(I32), 2 * TOK).then_inc(setup_pool, 1)
            pool.wait_ge(setup_pool, 4)
            pool.wait_ge(pad_ready, 1)
            for e in range(E):
                pool.indirect_dma_start(out=slots, out_offset=bass.IndirectOffsetOnAxis(padi[:, e:e + 1], 0),
                                        in_=padrow[:, :], in_offset=None).then_inc(pad_stored, 16)
            slots_complete(pool)

            def load(b):
                first = table(pool, 0, b, E * REG)
                pool.dma_start(brest[b.par], slots[bass.ds(first, P), D:ROW]).then_inc(rest_loaded[b.par], 16)

            for q in range(2):
                load(Batch(0, q))

            def body(b, ahead):
                q = b.par
                wait(pool, bo_ready, b, 1)
                apart(pool)
                pool.indirect_dma_start(out=out, out_offset=bass.IndirectOffsetOnAxis(brest[q][:, 2 * D:2 * D + 1].bitcast(I32), 0),
                                        in_=bo[q], in_offset=None, bounds_check=TOK - 1, oob_is_err=False).then_inc(row_out[q], 16)
                pool.wait_ge(row_out[q], b.i * 16 + 16)
                apart(pool)
                if ahead == 2:
                    load(b.plus(2))

            blocks(pool, body)

        block = ctx.enter_context(nc.Block())
        u_v = u.rearrange("b (c p) d -> b p c d", p=P)

        @block.sync
        def _(sp):
            ct_moved.start(sp)
            sp.dma_start(xin[0][:, :, :], u_v[0]).then_inc(x_loaded[0], 16)
            sp.dma_start(colp[:, :], cols_in).then_inc(consts_in_sb, 16)
            sp.dma_start(K[:, :], consts_in).then_inc(consts_in_sb, 16)
            sp.dma_start(cT[:, :, :], c_t).then_inc(consts_in_sb, 16)
            sp.dma_start(rowp[:, :], rows_in.partition_broadcast(P)).then_inc(consts_in_sb, 16)
            sp.dma_start(Wr[:, :, :], w_router).then_inc(consts_in_sb, 16)
            sp.dma_start(Wmod, w_mod).then_inc(consts_in_sb, 16)
            sp.dma_start(Win, w_in).then_inc(win_in, 16)
            sp.dma_start(Wout[:, :, :], w_out).then_inc(wout_in, 16)
            sp.dma_start(xin[1][:, :, :], u_v[1]).then_inc(x_loaded[1], 16)
            sp.dma_start(Ws[:, :], w_shared).then_inc(ws_in, 16)
            sp.wait_ge(mod_set, 3)
            sp.dma_start(mod_dram, mpre[:, :]).then_inc(mod_stored, 16)
            sp.wait_ge(mod_stored, 16)
            for q in range(2):
                sp.dma_start(mrow[q][:, :, :].rearrange("p m d -> p (m d)"),
                             mod_dram[q].partition_broadcast(P)).then_inc(mod_loaded[q], 16)

            def move_ct(n):
                wait(sp, xs_ready, n, 1)
                sp.dma_start(CT[n.par][0:NS, :], BCs[n.par][NS:2 * NS, :]).then_inc(ct_moved.sem, 16)

            move_ct(FIRST)
            sp.wait_ge(modmm_done, 1)
            sp.dma_start(We[:, 0:(E - LATE) * WE].rearrange("p (e n) -> p e n", n=WE), w_experts[:, 0:E - LATE, :]).then_inc(we_low, 16)

            def body(t, more):
                if t.n:
                    move_ct(t.n)
                if more:
                    b = t.b
                    wait(sp, x1_ready, b, NC)
                    sp.dma_start(xin[b.par][:, :, :],
                                 u_v[bass.ds(b.num(2), 1)].rearrange("a p c d -> (a p) c d")).then_inc(x_loaded[b.par], 16)
                    wait(sp, base_ready, b, NC)
                    apart(sp)
                    wait(sp, gbrow_ready, b, 1)
                    sp.dma_start(mrow[b.par][:, :, :].rearrange("p m d -> p (m d)"),
                                 mod_dram[bass.ds(b.num(2), 1), :].rearrange("a n -> (a n)")
                                 .partition_broadcast(P)).then_inc(mod_loaded[b.par], 16)

            turns(sp, body)
            sp.wait_ge(scan_over, 1)
            sp.dma_start(top.rearrange("p (e n) -> p e n", n=WE), w_experts[:, E - LATE:, :]).then_inc(we_high, 16)
            routed_sync(sp)

        @block.tensor
        def _(pe):
            for s in SLOTS:
                s.full.start(pe, 1)
                s.free.start(pe, 1)

            def project_hT(t):
                wait(pe, hn_ready, t.n, NC)
                for k in range(KD):
                    ps = opened(pe, t, f"AhT{k}")
                    for c in range(NC):
                        ins = pe.transpose(ps[:, c * P:(c + 1) * P], hn[:, c, k * P:(k + 1) * P], ident)
                    fill(f"AhT{k}", ins)

            def project_dt(t):
                wait(pe, hT_ready, t.n, KD)
                ps = opened(pe, t, "Adt")
                for c in range(NC):
                    for k in range(KD):
                        ins = pe.matmul(ps[:, c * H:(c + 1) * H], hT[:, k, c * P:(c + 1) * P],
                                        Win[:, k, NPROJ - H:NPROJ], start=(k == 0), stop=(k == KD - 1))
                fill("Adt", ins)

            def project_x(t, name, first):
                ps = opened(pe, t, name)
                for k in range(KD):
                    ins = pe.matmul(ps, Win[:, k, first:first + P], hT[:, k, :], start=(k == 0), stop=(k == KD - 1))
                fill(name, ins)

            def project_z(t, c):
                ps = opened(pe, t, f"Az{c}")
                for k in range(KD):
                    ins = pe.matmul(ps, hT[:, k, c * P:(c + 1) * P], Win[:, k, 0:DI], start=(k == 0), stop=(k == KD - 1))
                fill(f"Az{c}", ins)

            def turn_B(t):
                wait(pe, xs_ready, t.n, 1)
                ps = opened(pe, t, "AtB")
                apart(pe)
                for c in range(NC):
                    ins = pe.transpose(ps[:, c * NS:(c + 1) * NS], BCs[t.n.par][0:NS, c * P:(c + 1) * P], ident[0:NS, 0:NS])
                fill("AtB", ins)

            def turn_x(t, j):
                wait(pe, xs_ready, t.n, j + 2)
                ps = opened(pe, t, f"AtX{j}")
                for c in range(NC):
                    ins = pe.transpose(ps[:, c * P:(c + 1) * P], xs[j % 2][:, c * P:(c + 1) * P], ident)
                fill(f"AtX{j}", ins)

            def piece(t, k):
                if not t.n:
                    return
                if k == 0:
                    project_hT(t)
                elif k == 1:
                    project_dt(t)
                    project_x(t, "AxB", 2 * DI)
                elif k < 6:
                    project_x(t, f"Ax{k - 2}", DI + (k - 2) * P)
                else:
                    project_z(t, k - 6)
                if k == 4:
                    turn_B(t)
                if 5 <= k < 9:
                    turn_x(t, k - 5)

            def scan_1(t, c):
                b = t.b
                q = b.par
                cs = slice(c * P, (c + 1) * P)
                if c == 0:
                    pe.wait_ge(ct_moved.sem, ct_moved.at(b, 1))
                ps = opened(pe, t, f"g{c}")
                fill(f"g{c}", pe.matmul(ps[:, 0:P], BCs[q][0:NS, cs], CT[q][0:NS, cs], start=True, stop=True))
                wait(pe, arhs_ready, b, c + 1)
                ps = opened(pe, t, f"seg{c}")
                fill(f"seg{c}", pe.matmul(ps, GT, arhs[c][:, :, :].rearrange("p h l -> p (h l)"), start=True, stop=True))
                ps = opened(pe, t, f"cu{c}")
                for k, m in enumerate((LE, GT, ONE)):
                    ins = pe.matmul(ps[:, k * H:(k + 1) * H], m, da[q][:, c, :], start=True, stop=True)
                fill(f"cu{c}", ins)

            def scan_2(t, c):
                b = t.b
                q = b.par
                wait(pe, W_ready, b, c + 1)
                if c > 0:
                    wait(pe, S_ready, b, c)
                    ps = opened(pe, t, f"yo{c}")
                    fill(f"yo{c}", pe.matmul(ps, CT[q][0:NS, c * P:(c + 1) * P], St[:, :, :].rearrange("n h p -> n (h p)"), start=True, stop=True))
                if c == 0:
                    wait(pe, X_ready, b, H)
                ps = opened(pe, t, f"yd{c}")
                for h in range(H):
                    ins = pe.matmul(ps[:, h * HD:(h + 1) * HD], Wm[:, h, :], Xt[q][:, c, h * HD:(h + 1) * HD], start=True, stop=True)
                fill(f"yd{c}", ins)
                if c < NC - 1:
                    wait(pe, Bh_ready, b, c + 1)
                    ps = opened(pe, t, f"dS{c}")
                    for h in range(H):
                        ins = pe.matmul(ps[0:NS, h * HD:(h + 1) * HD], Bh[:, h, :], Xt[q][:, c, h * HD:(h + 1) * HD], start=True, stop=True)
                    fill(f"dS{c}", ins)

            def turn_y(t, c):
                wait(pe, yn_ready, t.b, c + 1)
                ps = opened(pe, t, f"yT{c}")
                for k in range(KI):
                    ins = pe.transpose(ps[:, k * P:(k + 1) * P], yn[c % 2][:, k * P:(k + 1) * P], ident)
                fill(f"yT{c}", ins)

            def project_y(t, c):
                wait(pe, yT_ready, t.b, c + 1)
                ps = opened(pe, t, f"op{c}")
                for k in range(KI):
                    ins = pe.matmul(ps[:, 0:D], yT[:, k, :], Wout[:, k, :], start=(k == 0), stop=(k == KI - 1))
                fill(f"op{c}", ins)

            def turn_h2(t, c):
                wait(pe, h2_ready, t.b, c + 1)
                ps = opened(pe, t, f"h2T{c}")
                for k in range(KD):
                    ins = pe.transpose(ps[:, k * P:(k + 1) * P], h2[:, c, k * P:(k + 1) * P], ident)
                fill(f"h2T{c}", ins)

            def gate_up(t, j):
                for name, first in ((f"Cg{j}", j * P), (f"Cu{j}", F + j * P)):
                    ps = opened(pe, t, name)
                    for k in range(KD):
                        ins = pe.matmul(ps, Wsg[:, k, first:first + P], h2T[:, k, :], start=(k == 0), stop=(k == KD - 1))
                    fill(name, ins)

            def mlp(t):
                b = t.b
                wait(pe, h2T_ready, b, NC)
                ps = opened(pe, t, "rt")
                for c in range(NC):
                    for k in range(KD):
                        ins = pe.matmul(ps[:, c * E:(c + 1) * E], h2T[:, k, c * P:(c + 1) * P], Wr[:, k, :], start=(k == 0), stop=(k == KD - 1))
                fill("rt", ins)
                gate_up(t, 0)
                gate_up(t, 1)
                wait(pe, onehot_ready, b, 1)
                ps = opened(pe, t, "rk")
                oh = onehot[:, :, :].rearrange("p c e -> p (c e)")
                pe.matmul(ps[:, 0:NC * E], LT, oh, start=True, stop=True)
                fill("rk", pe.matmul(ps[:, NC * E:2 * NC * E], ONE, oh, start=True, stop=True))
                gate_up(t, 2)
                gate_up(t, 3)
                wait(pe, hid_ready, b, KF)
                for c in range(NC):
                    ps = opened(pe, t, f"dn{c}")
                    for j in range(KF):
                        ins = pe.matmul(ps[:, 0:D], hid[:, j, c * P:(c + 1) * P], Wsd[:, j, :], start=(j == 0), stop=(j == KF - 1))
                    fill(f"dn{c}", ins)

            def body(t, more):
                scan_1(t, 0)
                for s in range(NC + 2):
                    if s < NC - 1:
                        scan_1(t, s + 1)
                    if 1 <= s < NC + 1:
                        turn_y(t, s - 1)
                    if s < NC + 1:
                        piece(t, 2 * s)
                    else:
                        piece(t, 2 * NC + 1)
                    if s < NC:
                        scan_2(t, s)
                    if 2 <= s:
                        turn_h2(t, s - 2)
                    if s < NC:
                        piece(t, 2 * s + 1)
                    if 1 <= s < NC + 1:
                        project_y(t, s - 1)
                mlp(t)

            pe.wait_ge(consts_in_sb, 96)
            pe.wait_ge(cs_done, 2)
            for j, n in enumerate(("W0", "W1")):
                for k in range(KD):
                    ins = pe.matmul(banks[n][0:NB, :], cTs[:, k, :], Wmod[:, k, (j + 1) * 512:(j + 2) * 512], start=(k == 0), stop=(k == KD - 1))
            for j in range(4):
                for k in range(KD):
                    ins = pe.matmul(M[:, j * NB:(j + 1) * NB], Wmod[:, k, j * P:(j + 1) * P], cTs[:, k, :], start=(k == 0), stop=(k == KD - 1))
            ins.then_inc(modmm_done, 1)
            pe.wait_ge(lnb_done, 1)
            pe.wait_ge(wout_in, 16)
            for k in range(KI):
                ins = pe.matmul(banks["YD"][:, 0:D], lnb_b[:, k, :], Wout[:, k, :], start=(k == 0), stop=(k == KI - 1))
            ins.then_inc(bmm_done, 1)
            pe.wait_ge(setup_ready, 1)
            pe.wait_ge(win_in, 16)
            pro = Turn(BEFORE, "pro")
            for k in range(2 * NC + 2):
                piece(pro, k)
            for s in SLOTS:
                rest = len([v for v in s.uses if v[0] != "A"])
                if rest and rest < len(s.uses):
                    pe.wait_ge(s.free.sem, s.free.at(BEFORE, len(s.uses) - rest))
                if rest:
                    pe.sem_inc(s.full.sem, rest)
                    pe.sem_inc(s.free.sem, rest)
            pe.wait_ge(ws_in, 16)
            turns(pe, body)
            routed_tensor(pe)

        @block.scalar
        def _(act):
            for cnt in BY_ACT:
                cnt.start(act)

            def evac_hT(t):
                wait(act, modb_ready, t.n, 1)
                for k in range(KD):
                    ps = filled(act, t, f"AhT{k}")
                    ins = act.activation(hT[:, k, :], ps, ACT.Identity, bias=modb[:, k:k + 1], scale=modb[:, 2 + k:3 + k])
                    empty(f"AhT{k}", ins)
                for k in range(KD):
                    emptied(act, t, f"AhT{k}")
                    act.sem_inc(hT_ready.sem, 1)

            def evac_x(t, q):
                name = "AxB" if q == 0 else f"Ax{q - 1}"
                j = (q - 1) % NT
                n = t.n
                ps = filled(act, t, name)
                wait(act, conv_ready, n, max(q - 1, 0))
                act.activation(xpre[q % 2][:, 3:], ps, ACT.Identity, bias=colp[:, IB + j:IB + j + 1]).then_inc(xpre_ready.sem, 1)
                wait(act, xpre_ready, n, q + 1)
                act.sem_inc(WHERE[name].free.sem, 1)
                wait(act, xs_ready, n, max(q - 1, 0))
                act.activation(acc[q % 2][:, :], xpre[q % 2][:, 0:SEQ], ACT.Identity, bias=colp[:, CB + j:CB + j + 1],
                               scale=colp[:, CW + 4 * j:CW + 4 * j + 1]).then_inc(tap_ready.sem, 1)

            def tanh_x(t, q):
                wait(act, conv_ready, t.n, q + 1)
                act.activation(th[q % 2][:, :], acc[q % 2][:, :], ACT.Tanh).then_inc(th_ready.sem, 1)

            def tanh_z(t, c):
                wait(act, zh_ready, t.n, c + 1)
                wait(act, z_ready, t.n, c - 1)
                act.activation(zth[c % 2][:, :], zh[c % 2][:, :], ACT.Tanh).then_inc(zth_ready.sem, 1)

            def piece(t, k):
                if not t.n:
                    return
                n = t.n
                if k == 0:
                    evac_hT(t)
                if k == 1:
                    evac_x(t, 0)
                if k == 2:
                    wait(act, dtx_ready, n, 1)
                    act.activation(dts[:, 2, :], dts[:, 1, :], ACT.Exp, scale=-1.0).then_inc(dte_ready.sem, 1)
                    evac_x(t, 1)
                if 3 <= k <= 5:
                    if k == 5:
                        ps = filled(act, t, "AtB")
                        empty("AtB", act.activation(Btok[n.par][:, :, :].rearrange("p c n -> p (c n)"), ps[:, 0:NC * NS], ACT.Copy))
                        emptied(act, t, "AtB")
                        act.sem_inc(btok_ready.sem, 1)
                    tanh_x(t, k - 3)
                    evac_x(t, k - 1)
                if k == 6:
                    tanh_x(t, 3)
                if k == 7:
                    tanh_x(t, 4)
                    tanh_z(t, 0)
                if k == 8:
                    tanh_z(t, 1)
                if k == 9:
                    tanh_z(t, 2)
                    tanh_z(t, 3)

            def exps(t, c):
                b = t.b
                ps = filled(act, t, f"seg{c}")
                wait(act, W_ready, b, c - 1)
                act.activation(Ex[c % 2][:, :, :].rearrange("p h l -> p (h l)"), ps, ACT.Exp).then_inc(E_ready.sem, 1)
                ps = filled(act, t, f"cu{c}")
                act.activation(ec[c][:, :], ps[:, 0:3 * H], ACT.Exp).then_inc(ec_ready.sem, 1)
                wait(act, E_ready, b, c + 1)
                wait(act, ec_ready, b, c + 1)
                act.sem_inc(SG.free.sem, 1)
                act.sem_inc(WHERE[f"cu{c}"].free.sem, 1)

            def norm_y(t, c):
                wait(act, y_stats, t.b, c + 1)
                act.activation(yn[c % 2][:, :], y[c % 2][:, :], ACT.Identity, bias=rs[c % 2][:, 1:2], scale=rs[c % 2][:, 0:1]).then_inc(yn_ready.sem, 1)

            def evac_yT(t, c):
                ps = filled(act, t, f"yT{c}")
                act.activation(yT[:, :, :].rearrange("p k n -> p (k n)"), ps, ACT.Copy).then_inc(yT_ready.sem, 1)
                wait(act, yT_ready, t.b, c + 1)
                act.sem_inc(WHERE[f"yT{c}"].free.sem, 1)

            def norm_x1(t, c):
                wait(act, x1_stats, t.b, c + 1)
                wait(act, h2_ready, t.b, c - 1)
                act.activation(n2[c % 2][:, :], rowbuf[:, c, D:2 * D], ACT.Identity, bias=rs2[c % 2][:, 1:2], scale=rs2[c % 2][:, 0:1]).then_inc(n2_ready.sem, 1)

            def evac_h2T(t, c):
                ps = filled(act, t, f"h2T{c}")
                act.activation(h2T[:, :, c * P:(c + 1) * P], ps[:, 0:KD * P].rearrange("p (k n) -> p k n", k=KD), ACT.Copy).then_inc(h2T_ready.sem, 1)
                wait(act, h2T_ready, t.b, c + 1)
                act.sem_inc(WHERE[f"h2T{c}"].free.sem, 1)

            def body(t, more):
                b = t.b
                exps(t, 0)
                for s in range(NC + 2):
                    if s < NC - 1:
                        exps(t, s + 1)
                    if 2 <= s:
                        norm_x1(t, s - 2)
                    if 1 <= s < NC + 1:
                        evac_yT(t, s - 1)
                    if s < NC + 1:
                        piece(t, 2 * s)
                    if 2 <= s:
                        evac_h2T(t, s - 2)
                    if s == NC + 1:
                        piece(t, 2 * NC + 1)
                    if s < NC:
                        piece(t, 2 * s + 1)
                        norm_y(t, s)
                wait(act, onehot_ready, b, 1)
                act.activation(mx[:, 1, :], mx[:, 0, :], ACT.Tanh, scale=0.5).then_inc(gth_ready.sem, 1)
                rows_left(act, b)
                act.wait_ge(mod_loaded[b.par], b.i * 16 + 16)
                for c in range(NC):
                    ins = act.activation(rowbuf[:, c, 2 * D:3 * D], mrow[b.par][:, 3, :], ACT.Copy)
                ins.then_inc(gbrow_ready.sem, 1)
                for j in range(KF):
                    ps = filled(act, t, f"Cg{j}")
                    wait(act, hid_ready, b, j - 1)
                    act.activation(th[j % 2][:, :], ps, ACT.Tanh, scale=0.5).then_inc(fth_ready.sem, 1)

            act.wait_ge(consts_in_sb, 96)
            act.activation(cth[:, :, :], cT[:, :, :], ACT.Tanh, scale=0.5).then_inc(cth_done, 1)
            act.activation(negA[:, :], rowp[:, AL:AL + H], ACT.Exp).then_inc(neg_done, 1)
            act.wait_ge(setup_ready, 1)
            pro = Turn(BEFORE, "pro")
            for k in range(2 * NC + 2):
                piece(pro, k)
            turns(act, body)
            routed_scalar(act)

        @block.vector
        def _(dve):
            for cnt in BY_DVE:
                cnt.start(dve)
            ca, cb_, cl = Chain(dve, dve_a), Chain(dve, dve_b), Chain(dve, dve_l)

            def ln1(b, count):
                cl.begin(b)
                dve.wait_ge(x_loaded[b.par], b.i * 16 + 16)
                wait(dve, hn_ready, b, 0)
                for c in range(NC):
                    ins = dve.bn_stats(st1[:, c, :], xin[b.par][:, c, :])
                cl.link(ins, apart)
                for c in range(NC):
                    ins = dve.bn_aggr(mv1[:, c, :], st1[:, c, :])
                cl.link(ins)
                dve.tensor_scalar(vl1[:, :], mv1[:, :, 1], EPS, None, ALU.add).then_inc(ln1_stats.sem, 1)
                cl.end()

            def dt_1(t):
                n = t.n
                ps = filled(dve, t, "Adt")
                v = dts[:, 0, :].rearrange("p (c h) -> p c h", c=NC)
                empty("Adt", dve.tensor_tensor(v, ps[:, 0:NC * H].rearrange("p (c h) -> p c h", c=NC),
                                               dtb[:, :].unsqueeze(1).broadcast_to([P, NC, H]), ALU.add))
                emptied(dve, t, "Adt")
                dve.scalar_tensor_tensor(out=dts[:, 1, :], in0=dts[:, 0, :], scalar=-1.0, in1=dts[:, 0, :],
                                         op0=ALU.mult, op1=ALU.max).then_inc(dtx_ready.sem, 1)

            def dt_2(t):
                n = t.n
                wait(dve, dte_ready, n, 1)
                d = [dts[:, k, :] for k in range(8)]
                ca.link(dve.tensor_scalar(d[3], d[2], 2.0, None, ALU.add))
                ca.link(dve.reciprocal(d[4], d[3]))
                ca.link(dve.tensor_tensor(d[5], d[2], d[4], ALU.mult))
                ca.link(dve.tensor_tensor(d[6], d[5], d[5], ALU.mult))
                ca.link(dve.tensor_scalar(d[7], d[6], 1.0 / (2 * LOG_TERMS - 1), None, ALU.mult))
                for k in range(LOG_TERMS - 2, 0, -1):
                    ca.link(dve.scalar_tensor_tensor(out=d[7], in0=d[7], scalar=1.0 / (2 * k + 1), in1=d[6], op0=ALU.add, op1=ALU.mult))
                ca.link(dve.scalar_tensor_tensor(out=d[7], in0=d[7], scalar=1.0, in1=d[5], op0=ALU.add, op1=ALU.mult))
                ca.link(dve.tensor_scalar(d[3], d[0], 0.0, None, ALU.max))
                v = lambda a: a.rearrange("p (c h) -> p c h", c=NC)
                ca.link(dve.scalar_tensor_tensor(out=dt[n.par][:, :, :], in0=v(d[7]), scalar=2.0, in1=v(d[3]), op0=ALU.mult, op1=ALU.add))
                dve.tensor_tensor(da[n.par][:, :, :], dt[n.par][:, :, :], negA[:, :].unsqueeze(1).broadcast_to([P, NC, H]),
                                  ALU.mult).then_inc(dt_ready.sem, 1)

            def conv(t, q):
                j = (q - 1) % NT
                wait(dve, tap_ready, t.n, q + 1)
                for k in (1, 2, 3):
                    ins = dve.scalar_tensor_tensor(out=acc[q % 2][:, :], in0=xpre[q % 2][:, k:k + SEQ],
                                                   scalar=colp[:, CW + 4 * j + k:CW + 4 * j + k + 1], in1=acc[q % 2][:, :],
                                                   op0=ALU.mult, op1=ALU.add)
                    if k < 3:
                        ca.link(ins)
                ins.then_inc(conv_ready.sem, 1)

            def finish_x(t, q):
                n = t.n
                wait(dve, th_ready, n, q + 1)
                if q == 0:
                    o = BCs[n.par][:, :]
                else:
                    o = xs[(q - 1) % 2][:, :]
                    if q >= 3:
                        filled(dve, t, f"AtX{q - 3}")
                dve.scalar_tensor_tensor(out=o, in0=th[q % 2][:, :], scalar=1.0, in1=acc[q % 2][:, :],
                                         op0=ALU.add, op1=ALU.mult).then_inc(xs_ready.sem, 1)

            def evac_X(t, j):
                n = t.n
                ps = filled(dve, t, f"AtX{j}")
                wait(dve, dt_ready, n, 1)
                dve.tensor_tensor(Xt[n.par][:, :, j * P:(j + 1) * P], ps.rearrange("p (c d) -> p c d", c=NC),
                                  dt[n.par][:, :, j:j + 1].broadcast_to([P, NC, P]), ALU.mult).then_inc(X_ready.sem, 1)
                wait(dve, X_ready, n, j + 1)
                dve.sem_inc(WHERE[f"AtX{j}"].free.sem, 1)

            def half_z(t, c):
                n = t.n
                ps = filled(dve, t, f"Az{c}")
                wait(dve, z_ready, n, c - 1)
                dve.scalar_tensor_tensor(out=zh[c % 2][:, :], in0=ps, scalar=0.5, in1=rowp[:, ZB:ZB + DI],
                                         op0=ALU.mult, op1=ALU.add).then_inc(zh_ready.sem, 1)
                wait(dve, zh_ready, n, c + 1)
                dve.sem_inc(WHERE[f"Az{c}"].free.sem, 1)

            def finish_z(t, c):
                n = t.n
                wait(dve, zth_ready, n, c + 1)
                dve.scalar_tensor_tensor(out=Zs[n.par][:, c, :], in0=zth[c % 2][:, :], scalar=1.0, in1=zh[c % 2][:, :],
                                         op0=ALU.add, op1=ALU.mult).then_inc(z_ready.sem, 1)

            def piece(t, k):
                if not t.n:
                    return
                if k == 0:
                    ca.begin(t.n)
                    wait(dve, hT_ready, t.n, 0)
                    dve.tensor_copy(modb[:, :], modc[:, :, bass.ds(t.n.num(), 1)].rearrange("p m a -> p (m a)")).then_inc(modb_ready.sem, 1)
                if k == 1:
                    dt_1(t)
                if k == 2:
                    conv(t, 0)
                    dt_2(t)
                if k == 3:
                    finish_x(t, 0)
                    conv(t, 1)
                if k == 4:
                    finish_x(t, 1)
                    conv(t, 2)
                if k == 5:
                    finish_x(t, 2)
                    conv(t, 3)
                if k == 6:
                    evac_X(t, 0)
                    finish_x(t, 3)
                    conv(t, 4)
                if k == 7:
                    evac_X(t, 1)
                    half_z(t, 0)
                    finish_x(t, 4)
                if k == 8:
                    evac_X(t, 2)
                    half_z(t, 1)
                    finish_z(t, 0)
                    evac_X(t, 3)
                if k == 9:
                    half_z(t, 2)
                    finish_z(t, 1)
                    half_z(t, 3)
                    finish_z(t, 2)
                    finish_z(t, 3)
                    ca.end()

            def mask_g(t, c):
                ps = filled(dve, t, f"g{c}")
                wait(dve, W_ready, t.b, c)
                empty(f"g{c}", dve.tensor_tensor(Gm[:, :], ps[:, 0:P], LE, ALU.mult))
                emptied(dve, t, f"g{c}")

            def mask_w(t, c):
                b = t.b
                wait(dve, E_ready, b, c + 1)
                dve.tensor_tensor(Wm[:, :, :], Ex[c % 2][:, :, :], Gm[:, :].unsqueeze(1).broadcast_to([P, H, P]), ALU.mult)\
                    .then_inc(W_ready.sem, 1)

            def combine(t, c):
                b = t.b
                q = c % 2
                yd = filled(dve, t, f"yd{c}")
                wait(dve, z_ready, b, c + 1)
                wait(dve, yn_ready, b, c - 1)
                if c > 0:
                    yo = filled(dve, t, f"yo{c}")
                    wait(dve, ec_ready, b, c + 1)
                    dve.tensor_tensor(y[q][:, :].rearrange("p (h d) -> p h d", h=H), yo.rearrange("p (h d) -> p h d", h=H),
                                      ec[c][:, 0:H].unsqueeze(2).broadcast_to([P, H, HD]), ALU.mult).then_inc(YO.free.sem, 1)
                    emptied(dve, t, f"yo{c}")
                    dve.tensor_tensor(y[q][:, :], y[q][:, :], yd, ALU.add).then_inc(YD.free.sem, 1)
                    emptied(dve, t, f"yd{c}")
                    cb_.link(dve.tensor_tensor(y[q][:, :], y[q][:, :], Zs[b.par][:, c, :], ALU.mult))
                else:
                    dve.tensor_tensor(y[q][:, :], yd, Zs[b.par][:, c, :], ALU.mult).then_inc(YD.free.sem, 1)
                    emptied(dve, t, f"yd{c}")
                if c < NC - 1:
                    ps = filled(dve, t, f"dS{c}")
                    if c == 0:
                        dve.tensor_copy(St[:, :, :].rearrange("n h p -> n (h p)"), ps[0:NS, :]).then_inc(S_ready.sem, 1)
                    else:
                        for h in range(H):
                            ins = dve.scalar_tensor_tensor(out=St[:, h, :], in0=St[:, h, :], scalar=ec[c][0:NS, 2 * H + h:2 * H + h + 1],
                                                           in1=ps[0:NS, h * HD:(h + 1) * HD], op0=ALU.mult, op1=ALU.add)
                        ins.then_inc(S_ready.sem, 1)
                    wait(dve, S_ready, b, c + 1)
                    dve.sem_inc(SG.free.sem, 1)
                cb_.link(dve.bn_stats(st[:, :], y[q][:, :]), apart)
                cb_.link(dve.bn_aggr(mvy[q][:, 0:2], st[:, :]))
                dve.tensor_scalar(mvy[q][:, 2:3], mvy[q][:, 1:2], EPS, None, ALU.add).then_inc(y_var.sem, 1)

            def residual(t, c):
                b = t.b
                q = c % 2
                x1 = rowbuf[:, c, D:2 * D]
                if c == 0:
                    wait(dve, xg_ready, b, 1)
                    rows_left(dve, b)
                ps = filled(dve, t, f"op{c}")
                empty(f"op{c}", dve.tensor_tensor(t1[:, :], ps[:, 0:D], mrow[b.par][:, 0, :], ALU.mult))
                emptied(dve, t, f"op{c}")
                dve.tensor_tensor(x1, t1[:, :], xin[b.par][:, c, :], ALU.add).then_inc(x1_ready.sem, 1)
                wait(dve, x1_ready, b, c + 1)
                wait(dve, n2_ready, b, c - 1)
                cb_.link(dve.bn_stats(st[:, :], x1), apart)
                cb_.link(dve.bn_aggr(mvx[q][:, 0:2], st[:, :]))
                dve.tensor_scalar(mvx[q][:, 2:3], mvx[q][:, 1:2], EPS, None, ALU.add).then_inc(x1_var.sem, 1)

            def route(t):
                b = t.b
                ps = filled(dve, t, "rt")
                empty("rt", dve.tensor_copy(lg[:, :, :].rearrange("p c e -> p (c e)"), ps[:, 0:NC * E]))
                emptied(dve, t, "rt")
                cb_.link(dve.tensor_reduce(mx[:, 0, :], lg[:, :, :], AX.X, ALU.max))
                cb_.link(dve.tensor_tensor(rt[:, 0], lg[:, :, :], mx[:, 0, :].unsqueeze(2).broadcast_to([P, NC, E]), ALU.is_equal))
                cb_.link(dve.tensor_tensor(rt[:, 1], rt[:, 0], K[:, C_TIE:C_TIE + E].unsqueeze(1).broadcast_to([P, NC, E]), ALU.mult))
                cb_.link(dve.tensor_reduce(mx[:, 2, :], rt[:, 1], AX.X, ALU.max))
                dve.tensor_tensor(onehot[:, :, :], rt[:, 1], mx[:, 2, :].unsqueeze(2).broadcast_to([P, NC, E]), ALU.is_equal)\
                    .then_inc(onehot_ready.sem, 1)

            def place(t):
                b = t.b
                wait(dve, gth_ready, b, 1)
                dve.tensor_scalar(mx[:, 3, :], mx[:, 1, :], 0.5, 0.5, ALU.mult, ALU.add).then_inc(gate_ready.sem, 1)
                ps = filled(dve, t, "rk")
                for c in range(NC):
                    cb_.link(dve.tensor_tensor(carry[:, c + 1, :], carry[:, c, :], ps[:, (NC + c) * E:(NC + c + 1) * E], ALU.add))
                empty("rk", dve.tensor_tensor(rt[:, 2], carry[:, 0:NC, :],
                                              ps[:, 0:NC * E].rearrange("p (c e) -> p c e", c=NC), ALU.add))
                emptied(dve, t, "rk")
                cb_.link(dve.tensor_copy(carry[:, 0, :], carry[:, NC, :]))
                cb_.link(dve.tensor_tensor(rt[:, 3], rt[:, 2], onehot[:, :, :], ALU.mult))
                cb_.link(dve.tensor_reduce(posf[:, :], rt[:, 3], AX.X, ALU.add))
                cb_.link(dve.tensor_copy(posi[:, :], posf[:, :]))
                dve.tensor_copy(rowbuf[:, :, 3 * D].bitcast(I32), tidf[:, :]).then_inc(pos_ready.sem, 1)
                wait(dve, pos_ready, b, 1)
                cb_.link(dve.tensor_scalar(tidf[:, :], tidf[:, :], float(SEQ), None, ALU.add))

            def hidden(t, j):
                b = t.b
                wait(dve, fth_ready, b, j + 1)
                g, up = WHERE[f"Cg{j}"], WHERE[f"Cu{j}"]
                empty(f"Cg{j}", dve.scalar_tensor_tensor(out=acc[j % 2][:, :], in0=th[j % 2][:, :], scalar=1.0, in1=g.ap,
                                                         op0=ALU.add, op1=ALU.mult))
                emptied(dve, t, f"Cg{j}")
                filled(dve, t, f"Cu{j}")
                dve.tensor_tensor(hid[:, j, :], acc[j % 2][:, :], up.ap, ALU.mult).then_inc(hid_ready.sem, 1)
                wait(dve, hid_ready, b, j + 1)
                dve.sem_inc(up.free.sem, 1)

            def base(t, c):
                b = t.b
                ps = filled(dve, t, f"dn{c}")
                empty(f"dn{c}", dve.scalar_tensor_tensor(out=t1[:, :], in0=ps[:, 0:D], scalar=0.5, in1=mrow[b.par][:, 3, :],
                                                         op0=ALU.mult, op1=ALU.mult))
                emptied(dve, t, f"dn{c}")
                dve.tensor_tensor(rowbuf[:, c, D:2 * D], rowbuf[:, c, D:2 * D], t1[:, :], ALU.add).then_inc(base_ready.sem, 1)
                wait(dve, base_ready, b, c + 1)

            def body(t, more):
                b = t.b
                cb_.begin(b)
                dve.wait_ge(mod_loaded[b.par], b.i * 16 + 16)
                dve.tensor_tensor(gab[:, :], mrow[b.par][:, 0, :], brow[:, :], ALU.mult).then_inc(gab_ready.sem, 1)
                mask_g(t, 0)
                mask_w(t, 0)
                for s in range(NC + 2):
                    if s < NC - 1:
                        mask_g(t, s + 1)
                    if s < NC + 1:
                        piece(t, 2 * s)
                    else:
                        piece(t, 2 * NC + 1)
                    if s < NC:
                        combine(t, s)
                        if t.mode == "last" and s == NC - 1:
                            dve.sem_inc(scan_over, 1)
                        if s < NC - 1:
                            mask_w(t, s + 1)
                        piece(t, 2 * s + 1)
                    if 1 <= s < NC + 1:
                        residual(t, s - 1)
                route(t)
                hidden(t, 0)
                place(t)
                hidden(t, 1)
                if more:
                    ln1(Batch(b.i + 1, b.par), None)
                hidden(t, 2)
                hidden(t, 3)
                for c in range(NC):
                    base(t, c)
                cb_.end()

            steps = [0]

            def link(ins):
                steps[0] += 1
                ins.then_inc(setup_dve, 1)
                dve.wait_ge(setup_dve, steps[0])

            dve.wait_ge(consts_in_sb, 96)
            dve.wait_ge(cth_done, 1)
            dve.scalar_tensor_tensor(out=cTs[:, :, :], in0=cth[:, :, :], scalar=1.0, in1=cT[:, :, :], op0=ALU.add, op1=ALU.mult).then_inc(cs_done, 1)
            dve.wait_ge(cs_done, 1)
            dve.tensor_scalar(cTs[:, :, :], cTs[:, :, :], 0.5, None, ALU.mult).then_inc(cs_done, 1)
            for k in range(KI):
                ins = dve.tensor_scalar(lnb_b[:, k, :], ONE, colp[:, LB + k:LB + k + 1], None, ALU.mult)
            ins.then_inc(lnb_done, 1)
            link(dve.tensor_scalar(colp[:, CW:CW + 4 * NT + NT], colp[:, CW:CW + 4 * NT + NT], 0.5, None, ALU.mult))
            link(dve.tensor_scalar(rowp[:, ZB:ZB + DI], rowp[:, ZB:ZB + DI], 0.5, None, ALU.mult))
            link(dve.tensor_tensor(dtb[:, :], rowp[:, DTB:DTB + H], rowp[:, DTB2:DTB2 + H], ALU.add))
            dve.wait_ge(neg_done, 1)
            link(dve.tensor_scalar(negA[:, :], negA[:, :], -1.0, None, ALU.mult))
            link(dve.tensor_copy(carry[:, 0, :], K[:, C_REG:C_REG + E]))
            link(dve.tensor_copy(tidf[:, :], K[:, C_TID:C_TID + NC]))
            for q in range(2):
                ins = dve.memset(xpre[q][:, 0:3], 0.0)
            link(ins)
            dve.wait_ge(modmm_done, 1)
            link(dve.tensor_copy(modc[:, 0:2, :].rearrange("p m b -> p (m b)"), M[:, 0:2 * NB]))
            link(dve.tensor_scalar(modc[:, 2:4, :].rearrange("p m b -> p (m b)"), M[:, 2 * NB:4 * NB], 1.0, None, ALU.add))
            ga, sb_, cbm, gb = banks["W0"][0:NB, 0:D], banks["W0"][0:NB, D:2 * D], banks["W1"][0:NB, 0:D], banks["W1"][0:NB, D:2 * D]
            for k, g in enumerate((ga, gb)):
                m = mabs[:, k * D:(k + 1) * D]
                link(dve.tensor_scalar(m, g, -1.0, None, ALU.mult))
                link(dve.scalar_tensor_tensor(out=m, in0=m, scalar=0.25, in1=g, op0=ALU.max, op1=ALU.max))
                link(dve.tensor_scalar(msgn[:, k * D:(k + 1) * D], g, 0.0, 2.0, ALU.is_ge, ALU.mult))
                dve.scalar_tensor_tensor(out=mpre[:, 3 * k * D:(3 * k + 1) * D], in0=msgn[:, k * D:(k + 1) * D], scalar=-1.0,
                                         in1=mabs[:, k * D:(k + 1) * D], op0=ALU.add, op1=ALU.mult).then_inc(mod_set, 1)
            link(dve.tensor_scalar(mpre[:, D:2 * D], cbm, 1.0, None, ALU.add))
            dve.tensor_copy(mpre[:, 2 * D:3 * D], sb_).then_inc(mod_set, 1)
            dve.wait_ge(bmm_done, 1)
            link(dve.tensor_tensor(brow[:, :], banks["YD"][:, 0:D], rowp[:, OB:OB + D], ALU.add))
            for k in range(KI):
                ins = dve.tensor_scalar(Wout[:, k, :], Wout[:, k, :], colp[:, LW + k:LW + k + 1], None, ALU.mult)
            link(ins)
            dve.wait_ge(mod_set, 3)
            dve.sem_inc(setup_ready, 1)
            ln1(FIRST, None)
            pro = Turn(BEFORE, "pro")
            for k in range(2 * NC + 2):
                piece(pro, k)
                if k == 2:
                    ln1(Batch(0, 1), None)
            turns(dve, body)
            routed_vector(dve)

        @block.gpsimd
        def _(pool):
            for cnt in BY_POOL:
                cnt.start(pool)

            def normalise(b, before):
                wait(pool, ln1_stats, b, 1)
                if before:
                    filled(pool, before, "AhT1")
                pool.tensor_tensor(rs1[:, :], vl1[:, :], power[:, :], ALU.pow).then_inc(ln1_power.sem, 1)
                wait(pool, ln1_power, b, 1)
                apart(pool)
                for c in range(NC):
                    pool.tensor_scalar(hn[:, c, :], xin[b.par][:, c, :], mv1[:, c, 0:1], rs1[:, c:c + 1],
                                       ALU.subtract, ALU.mult).then_inc(hn_ready.sem, 1)

            def deviation(b, c, var, mvs, rss, powered, done):
                q = c % 2
                wait(pool, var, b, c + 1)
                pool.tensor_tensor(rss[q][:, 0:1], mvs[q][:, 2:3], power[:, 0:1], ALU.pow).then_inc(powered.sem, 1)
                wait(pool, powered, b, c + 1)
                apart(pool)
                pool.tensor_scalar(rss[q][:, 1:2], mvs[q][:, 0:1], rss[q][:, 0:1], -1.0, ALU.mult, ALU.mult).then_inc(done.sem, 1)

            def masked_a(t, c):
                n = t.n
                wait(pool, dt_ready, n, 1)
                if t.mode != "pro":
                    filled(pool, t, f"seg{c}")
                pool.tensor_tensor(arhs[c][:, :, :], LE.unsqueeze(1).broadcast_to([P, H, P]),
                                   da[n.par][:, c, :].unsqueeze(2).broadcast_to([P, H, P]), ALU.mult).then_inc(arhs_ready.sem, 1)

            def scale_B(t, c):
                b = t.b
                wait(pool, ec_ready, b, c + 1)
                if c == 0:
                    wait(pool, btok_ready, b, 1)
                pool.tensor_tensor(Bh[:, :, :], Btok[b.par][:, c, :].unsqueeze(1).broadcast_to([P, H, NS]),
                                   ec[c][:, H:2 * H].unsqueeze(2).broadcast_to([P, H, NS]), ALU.mult).then_inc(Bh_ready.sem, 1)

            def modulate(t, c):
                b = t.b
                wait(pool, n2_ready, b, c + 1)
                pool.tensor_tensor(h2[:, c, :], n2[c % 2][:, :], mrow[b.par][:, 1, :], ALU.mult).then_inc(h2_scaled.sem, 1)
                wait(pool, h2_scaled, b, c + 1)
                pool.tensor_tensor(h2[:, c, :], h2[:, c, :], mrow[b.par][:, 2, :], ALU.add).then_inc(h2_ready.sem, 1)

            def body(t, more):
                b = t.b
                pool.wait_ge(mod_loaded[b.par], b.i * 16 + 16)
                wait(pool, gab_ready, b, 1)
                scale_B(t, 0)
                pool.tensor_tensor(xin[b.par][:, :, :], xin[b.par][:, :, :], gab[:, :].unsqueeze(1).broadcast_to([P, NC, D]),
                                   ALU.add).then_inc(xg_ready.sem, 1)
                for s in range(NC + 2):
                    if 2 <= s:
                        modulate(t, s - 2)
                        if t.n:
                            masked_a(t, s - 2)
                    if s < NC:
                        deviation(b, s, y_var, mvy, rs, y_power, y_stats)
                    if s < NC - 2:
                        scale_B(t, s + 1)
                    if 1 <= s < NC + 1:
                        deviation(b, s - 1, x1_var, mvx, rs2, x1_power, x1_stats)
                wait(pool, gate_ready, b, 1)
                apart(pool)
                for c in range(NC):
                    pool.tensor_scalar(rowbuf[:, c, 0:D], h2[:, c, :], mx[:, 3, c:c + 1], None, ALU.mult).then_inc(h2g_ready.sem, 1)
                if more:
                    normalise(Batch(b.i + 1, b.par), t)
                wait(pool, pos_ready, b, 1)
                wait(pool, gbrow_ready, b, 1)
                wait(pool, h2g_ready, b, NC)
                for c in range(NC):
                    wait(pool, base_ready, b, c + 1)
                    apart(pool)
                    pool.indirect_dma_start(out=slots, out_offset=bass.IndirectOffsetOnAxis(posi[:, c:c + 1], 0),
                                            in_=rowbuf[:, c, :], in_offset=None).then_inc(scattered, 16)

            pool.memset(rowbuf[:, 0, :], 0.0).then_inc(setup_pool, 1)
            pool.wait_ge(setup_pool, 1)
            pool.memset(rowbuf[:, 0, 3 * D:].bitcast(I32), 2 * TOK).then_inc(setup_pool, 1)
            pool.wait_ge(setup_pool, 2)
            pool.dma_start(slots[E * REG:, :], rowbuf[:, 0, :]).then_inc(scattered, 16)
            pool.memset(power[:, :], -0.5).then_inc(power_set, 1)
            pool.wait_ge(power_set, 1)
            pro = Turn(BEFORE, "pro")
            normalise(FIRST, None)
            normalise(Batch(0, 1), pro)
            for c in range(NC):
                masked_a(pro, c)
            turns(pool, body)
            routed_gpsimd(pool)


def kernel(**inputs):
    import numpy as np
    import concourse.bacc as bacc
    from concourse.bass_utils import run_bass_kernel_spmd as run

    g = {k: np.asarray(v) for k, v in inputs.items()}

    def tiles(w):
        return np.ascontiguousarray(w.reshape(-1, P, w.shape[-1]).transpose(1, 0, 2))

    def expert(gu, down):
        return np.concatenate([tiles(gu).reshape(P, -1), tiles(down).reshape(P, -1)], 1)

    cols = np.concatenate([
        g["L0_attn_conv_w"].reshape(NT, P, 4).transpose(1, 0, 2).reshape(P, -1),
        g["L0_attn_conv_b"].reshape(NT, P).T,
        g["L0_attn_in_proj_b"][DI:DI + NT * P].reshape(NT, P).T,
        g["L0_attn_ln_w"].reshape(KI, P).T, g["L0_attn_ln_b"].reshape(KI, P).T], 1)
    rows = np.concatenate([g["L0_attn_in_proj_b"][:DI], g["L0_attn_in_proj_b"][NPROJ - H:], g["L0_attn_dt_bias"],
                           g["L0_attn_A_log"], g["L0_attn_out_proj_b"]])
    k = np.zeros((P, NCONST), np.float32)
    r = np.arange(P)
    k[:, C_ID:C_ID + P] = r[:, None] == r
    k[:, C_LE:C_LE + P] = r[:, None] <= r
    k[:, C_GT:C_GT + P] = r[:, None] > r
    k[:, C_LT:C_LT + P] = r[:, None] < r
    k[:, C_ONE:C_ONE + P] = 1
    e, i = np.arange(E), np.arange(NBLK)
    k[:, C_TIE:C_TIE + E] = E - e
    k[:, C_REG:C_REG + E] = e * REG
    k[:, C_TID:C_TID + NC] = r[:, None] + P * np.arange(NC)
    k[:, C_P] = r
    k[:, C_CMP:C_CMP + TOK // P] = P * np.arange(TOK // P)
    k[:, C_I:C_I + NBLK * E] = np.repeat(i, E)
    k[:, C_OFF:C_OFF + NBLK * E] = (i[:, None] * P + (e - E) * REG).reshape(-1)
    k[:, C_E:C_E + E] = e * WE
    arrays = {
        "u": g["L0_attn_u"],
        "w_in": tiles(g["L0_attn_in_proj_w"].T), "w_out": tiles(g["L0_attn_out_proj_w"].T),
        "w_router": tiles(g["L0_ffn_router_w"].T), "w_mod": tiles(g["L0_wmod"]), "c_t": tiles(g["L0_c"].T),
        "w_experts": np.stack([expert(a, b) for a, b in zip(g["L0_ffn_w_gate_up"], g["L0_ffn_w_down"])], 1),
        "w_shared": expert(g["L0_ffn_shared_gate_up"], g["L0_ffn_shared_down"]),
        "cols_in": cols, "rows_in": rows, "consts_in": k,
    }
    arrays = {n: np.ascontiguousarray(a) for n, a in arrays.items()}
    nc = bacc.Bacc("TRN2", target_bir_lowering=False, num_devices=1)
    args = [nc.dram_tensor(n, a.shape, mybir.dt.from_np(a.dtype), kind="ExternalInput").ap() for n, a in arrays.items()]
    args.append(nc.dram_tensor("result", (TOK, D), F32, kind="ExternalOutput").ap())
    build(nc, *args)
    r = run(nc, [arrays], core_ids=[0])
    return r.results[0]["result"].reshape(NB, SEQ, D)
```

```python
from contextlib import ExitStack

import concourse.bass as bass
from concourse import mybir

F32 = mybir.dt.float32
I32 = mybir.dt.int32
ALU = mybir.AluOpType
ACT = mybir.ActivationFunctionType
AX = mybir.AxisListType

P = 128
NB, SEQ, D = 8, 512, 256
NC = SEQ // P
H, HD, NS = 4, 128, 64
DI = H * HD
NT = 5
NPROJ = 2 * DI + 2 * NS + H
E, F = 8, 512
KD, KF, KI = D // P, F // P, DI // P
WE = KD * 2 * F + KF * D
TOK = NB * SEQ
REG = TOK + P
NBLK = TOK // P + E - 1
ROW = 3 * D + 1
LATE = 7
EPS = 1e-5
LOG_TERMS = 9

CW, CB, IB, LW, LB = 0, 20, 25, 30, 34
NCOL = 38
ZB, DTB, DTB2, AL, OB = 0, 512, 516, 520, 524
NROW = 780
C_ID, C_LE, C_GT, C_LT, C_ONE = (k * P for k in range(5))
C_TIE = 5 * P
C_REG = C_TIE + E
C_TID = C_REG + E
C_P = C_TID + NC
C_CMP = C_P + 1
C_I = C_CMP + TOK // P
C_OFF = C_I + NBLK
C_E = C_OFF + NBLK * E
NCONST = C_E + E

T_ORDER = ["cu", "AtB", "AtX0", "yT0", "AtX1", "yT1", "AtX2", "h2T0", "yT2", "AtX3",
           "h2T1", "yT3", "h2T2", "EhT0", "EhT1", "h2T3", "dn0", "dn1", "dn2", "dn3"]
W_ORDER = ["Ax2", "Ax3", "Az0", "Az1", "Az2", "Az3", "ExB", "Cg0", "Cu0", "Cg2", "Cu2", "Ex0", "Ex1"]
EARLY_X = 3


class Batch:

    def __init__(self, i, par):
        self.i, self.par = i, par

    def next(self):
        return Batch(self.i, 1) if self.par == 0 else Batch(self.i + 1, 0)

    def plus(self, k):
        return self if k == 0 else self.next().plus(k - 1)

    def num(self, add=0):
        return self.i * 2 + (self.par + add)


class Count:

    def __init__(self, sem, per, step=1):
        self.sem, self.per, self.step = sem, per, step

    def at(self, b, k):
        return b.i * (2 * self.per * self.step) + (self.per * b.par + k + 2 * self.per) * self.step

    def start(self, eng, batches=2):
        eng.sem_inc(self.sem, batches * self.per * self.step)


class Slot:

    def __init__(self, ap, full, free, uses):
        self.ap, self.uses = ap, uses
        self.full, self.free = Count(full, len(uses)), Count(free, len(uses))

        self.late, self.soon = (sum(u[0] == k for u in uses) for k in "AE")

    def credit(self):
        return 2 * len(self.uses) - self.late - 2 * self.soon

    def index(self, use, mode):
        kinds, shift = {
            "pro2": ("E", self.credit()),
            "pro1": ("AE", len(self.uses) - self.late - self.soon),
            "full": (None, 0),
            "no_early": (None, 0),
            "last": (None, -self.soon)}[mode]
        some = [u for u in self.uses if kinds is None or u[0] in kinds]
        if mode in ("no_early", "last"):
            some = [u for u in some if u[0] != "E" and (mode == "no_early" or u[0] != "A")]
        return some.index(use) + shift


class Turn:

    def __init__(self, b, mode):
        self.b, self.mode, self.n = b, mode, None

    def projecting(self, k):
        if (k == 1 and self.mode in ("last", "pro2")) or (k == 2 and self.mode in ("last", "no_early")):
            return None
        t = Turn(self.b, self.mode)
        t.n = self.b.plus(k)
        return t


class Chain:

    def __init__(self, eng, count):
        self.eng, self.count, self.k, self.b = eng, count, 0, None

    def begin(self, b, k=0):
        self.b, self.k = b, k

    def link(self, ins, apart=None):
        self.k += 1
        ins.then_inc(self.count.sem, 1)
        self.eng.wait_ge(self.count.sem, self.count.at(self.b, self.k))
        if apart:
            apart(self.eng)

    def end(self, k=None):
        assert self.k == (self.count.per if k is None else k), ("steps of this chain in a batch", self.k)


def build(nc, u, w_in, w_out, w_router, w_mod, c_t, w_experts, w_shared, cols_in, rows_in, consts_in, out):
    ctx = ExitStack()
    with ctx:
        def sb(name, shape, dt=F32):
            return ctx.enter_context(nc.sbuf_tensor(name, shape, dt))

        def sem(name):
            return ctx.enter_context(nc.semaphore(name))

        slots = nc.dram_tensor("slots", (E * REG + P, ROW), F32, kind="Internal").ap()
        mod_dram = nc.dram_tensor("mod_rows", (NB, 4 * D), F32, kind="Internal").ap()

        We = sb("We", [P, E * WE])
        top = We[:, (E - LATE) * WE:]
        used = [0]

        def early(n):
            used[0] += n
            assert used[0] <= LATE * WE
            return top[:, used[0] - n:used[0]]

        Ws = sb("Ws", [P, WE])
        Wsg = Ws[:, 0:KD * 2 * F].rearrange("p (k n) -> p k n", k=KD)
        Wsd = Ws[:, KD * 2 * F:].rearrange("p (k n) -> p k n", k=KF)
        Xt = [early(NC * DI).rearrange("p (c n) -> p c n", c=NC) for _ in range(2)]
        Zs = [early(NC * DI).rearrange("p (c n) -> p c n", c=NC) for _ in range(2)]
        Win = early(KD * NPROJ).rearrange("p (k n) -> p k n", k=KD)
        xpre = [early(3 + SEQ) for _ in range(2)]
        Wout = sb("Wout", [P, KI, D])
        Wr = sb("Wr", [P, KD, E])
        Wmod = We[:, 0:KD * 6 * D].rearrange("p (k n) -> p k n", k=KD)
        colp = sb("colp", [P, NCOL])
        rowp = sb("rowp", [P, NROW])
        K = sb("K", [P, NCONST])
        ident, LE, GT, LT, ONE = (K[:, c:c + P] for c in (C_ID, C_LE, C_GT, C_LT, C_ONE))
        cT = sb("cT", [P, KD, NB])
        cTs = sb("cTs", [P, KD, NB])
        cth = sb("cth", [P, KD, NB])
        modc = sb("modc", [P, 4, NB])
        modb = sb("modb", [P, 4])
        brow = sb("brow", [P, D])
        negA = sb("negA", [P, H])
        dtb = sb("dtb", [P, H])

        xin = [sb(f"xin{q}", [P, NC, D]) for q in range(2)]
        mrow = [sb(f"mrow{q}", [P, 4, D]) for q in range(2)]
        gab = sb("gab", [P, D])
        hn = sb("hn", [P, NC, D])
        hT = sb("hT", [P, KD, SEQ])
        acc = [sb(f"acc{q}", [P, SEQ]) for q in range(2)]
        th = [sb(f"th{q}", [P, SEQ]) for q in range(2)]
        cacc = [early(SEQ), sb("cacc1", [P, SEQ])]
        ctanh = [sb(f"ctanh{q}", [P, SEQ]) for q in range(2)]
        xs = [early(SEQ) for _ in range(2)]
        BCs = [early(SEQ) for _ in range(2)]
        CT = [early(SEQ) for _ in range(2)]
        Btok = [early(NC * NS).rearrange("p (c n) -> p c n", c=NC), sb("Btok1", [P, NC, NS])]
        zh = [early(DI) for _ in range(2)]
        zth = [early(DI) for _ in range(2)]
        dts = sb("dts", [P, 8, NC * H])
        dt = [sb(f"dt{q}", [P, NC, H]) for q in range(2)]
        da = [sb(f"da{q}", [P, NC, H]) for q in range(2)]
        arhs = [early(H * P).rearrange("p (h l) -> p h l", h=H) for _ in range(NC)]
        Ex = [early(H * P).rearrange("p (h l) -> p h l", h=H) for _ in range(2)]
        ec = sb("ec", [P, 3, NC, H])
        Gm = early(P)
        Wm = early(H * P).rearrange("p (h l) -> p h l", h=H)
        Bh = early(H * NS).rearrange("p (h n) -> p h n", h=H)
        St = sb("St", [NS, H, HD])
        y = [sb(f"y{q}", [P, DI]) for q in range(2)]
        yn = [sb(f"yn{q}", [P, DI]) for q in range(2)]
        yT = sb("yT", [P, KI, P])
        t1 = sb("t1", [P, D])
        st = sb("st", [P, 6])
        mvy = [sb(f"mvy{q}", [P, 3]) for q in range(2)]
        mvx = [sb(f"mvx{q}", [P, 3]) for q in range(2)]
        power = sb("power", [P, NC])
        vl1 = sb("vl1", [P, NC])
        rs = [sb(f"ry{q}", [P, 2]) for q in range(2)]
        rs2 = [sb(f"rx{q}", [P, 2]) for q in range(2)]
        st1 = sb("st1", [P, NC, 6])
        mv1 = sb("mv1", [P, NC, 2])
        rs1 = sb("rs1", [P, NC])
        nm1 = sb("nm1", [P, NC])
        nb1 = sb("nb1", [P, NC])
        n2 = [sb(f"n2{q}", [P, D]) for q in range(2)]
        h2 = sb("h2", [P, NC, D])
        h2T = sb("h2T", [P, KD, SEQ])
        rowbuf = sb("rowbuf", [P, NC, ROW])
        hid = sb("hid", [P, KF, SEQ])
        lg = sb("lg", [P, NC, E])
        rt = sb("rt", [P, 4, NC, E])
        mx = sb("mx", [P, 4, NC])
        onehot = sb("onehot", [P, NC, E])
        carry = sb("carry", [P, NC + 1, E])
        posf = sb("posf", [P, NC])
        posi = sb("posi", [P, NC], I32)
        tidf = sb("tidf", [P, NC])
        padf = sb("padf", [P, E])
        padi = sb("padi", [P, E], I32)
        tab = sb("tab", [P, 6, E])
        tabr = sb("tabr", [P, 2, NBLK])
        tabi = sb("tabi", [P, 2, NBLK], I32)

        mpre = h2T[0:NB, :, :].rearrange("b k n -> b (k n)")
        mabs, msgn = hid[0:NB, 0, :], hid[0:NB, 1, :]
        lnb_b = hid[:, 2, :].rearrange("p (k n) -> p k n", k=KI)
        padrow = xin[0][:, :, :].rearrange("p c d -> p (c d)")[:, 0:ROW]
        tabj = hn[:, 0, 0:E * (TOK // P)].rearrange("p (e j) -> p e j", e=E)
        tabb = xin[1][:, :, :].rearrange("p c d -> p (c d)")[:, 0:3 * NBLK * E].rearrange("p (m i e) -> p m i e", m=3, e=E)

        bx = [hn[:, q, :] for q in range(2)]
        brest = [rowbuf[:, 2 * q, 0:2 * D + 1] for q in range(2)]
        bxT = [h2T[:, :, q * P:(q + 1) * P] for q in range(2)]
        bth = [th[q][:, :] for q in range(2)]
        bhg = [acc[q][:, :] for q in range(2)]
        bhid = [y[q][:, :] for q in range(2)]
        bhT = [yn[q][:, :].rearrange("p (k n) -> p k n", k=KF) for q in range(2)]
        bt = [n2[q][:, :] for q in range(2)]
        bo = [h2[:, q, :] for q in range(2)]

        def pb(name):
            return ctx.enter_context(nc.psum_tensor(name, [P, 512], F32))

        banks = {n: pb("ps" + n) for n in ("T0", "T1", "W0", "W1", "SG", "YD", "YO", "M")}

        def slot(name, ap, uses):
            return Slot(ap, sem(f"{name}_full"), sem(f"{name}_free"), uses)

        T = [slot(f"T{q}", banks[f"T{q}"][:, :], T_ORDER[q::2]) for q in range(2)]
        W = [slot(f"W{q}", banks[f"W{q}"][:, :], W_ORDER[q::2]) for q in range(2)]
        SG = slot("SG", banks["SG"][:, :], ["seg0"] + [f"{w}{c + k}" for c in range(NC - 1) for k, w in ((1, "seg"), (0, "dS"))])
        YD = slot("YD", banks["YD"][:, :], [f"yd{c}" for c in range(NC)] + ["Cg1", "Cg3"])
        YO = slot("YO", banks["YO"][:, :], ["g0", "g1"] + [f"{w}{c + k}" for c in range(1, NC - 1) for k, w in ((1, "g"), (0, "yo"))] + [f"yo{NC - 1}", "Cu1", "Cu3"])
        M = banks["M"]
        MM = slot("M", M[:, :], ["op0", "op1", "op2", "op3", "rt", "Edt", "rk"])
        SLOTS = [*T, *W, SG, YD, YO, MM]
        WHERE = {use: s for s in SLOTS for use in s.uses}

        def count(name, per, step=1):
            return Count(sem(name), per, step)

        hn_loaded = sem("hn_loaded")
        x_loaded = [sem("x_loaded0"), sem("x_loaded1")]
        mod_loaded = [sem("mod_loaded0"), sem("mod_loaded1")]
        ct_moved = [sem("ct_moved0"), sem("ct_moved1")]
        scattered = sem("scattered")
        hn_ready = count("hn_ready", NC)
        hT_ready = count("hT_ready", KD)
        xpre_ready = count("xpre_ready", NT)
        tap_ready = count("tap_ready", NT)
        th_ready = count("th_ready", NT)
        X_ready = count("X_ready", H)
        zth_ready = count("zth_ready", NC)
        dte_ready = count("dte_ready", 1)
        btok_ready = count("btok_ready", 1)
        E_ready = count("E_ready", NC)
        ec_ready = count("ec_ready", 1)
        yn_ready = count("yn_ready", NC)
        yo_ready = count("yo_ready", NC - 1)
        yT_ready = count("yT_ready", NC)
        n2_ready = count("n2_ready", NC)
        h2T_ready = count("h2T_ready", NC)
        gth_ready = count("gth_ready", 1)
        gbrow_ready = count("gbrow_ready", 1)
        fth_ready = count("fth_ready", KF)
        dve_a = count("dve_a", 6 + LOG_TERMS + 2 * NT)
        dve_b = count("dve_b", 6 * NC + 8)
        dve_l = count("dve_l", 2)
        dtx_ready = count("dtx_ready", 1)
        dt_ready = count("dt_ready", 1)
        conv_ready = count("conv_ready", NT)
        xs_ready = count("xs_ready", NT)
        zh_ready = count("zh_ready", NC)
        W_ready = count("W_ready", NC)
        y_var = count("y_var", NC)
        x1_var = count("x1_var", NC)
        x1_ready = count("x1_ready", NC)
        modb_ready = count("modb_ready", 1)
        gab_ready = count("gab_ready", 1)
        ln1_stats = count("ln1_stats", 1)
        onehot_ready = count("onehot_ready", 1)
        gate_ready = count("gate_ready", 1)
        pos_ready = count("pos_ready", 1)
        hid_ready = count("hid_ready", KF)
        base_ready = count("base_ready", NC)
        S_ready = count("S_ready", NC - 1)
        z_ready = count("z_ready", NC)
        S_decayed = count("S_decayed", NC - 2)
        y_power = count("y_power", NC)
        y_stats = count("y_stats", NC)
        x1_power = count("x1_power", NC)
        x1_stats = count("x1_stats", NC)
        ln1_power = count("ln1_power", 1)
        ln1_dev = count("ln1_dev", 1)
        arhs_ready = count("arhs_ready", NC)
        Bh_ready = count("Bh_ready", NC - 1)
        xg_ready = count("xg_ready", 1)
        h2_scaled = count("h2_scaled", NC)
        h2_ready = count("h2_ready", NC)
        h2g_ready = count("h2g_ready", 1)
        BY_ACT = [hn_ready, yo_ready, X_ready, hT_ready, xpre_ready, tap_ready, th_ready, zth_ready, dte_ready, btok_ready, E_ready,
                  ec_ready, yn_ready, yT_ready, n2_ready, h2T_ready, gth_ready, gbrow_ready, fth_ready]
        BY_DVE = [dve_a, dve_b, dve_l, dtx_ready, dt_ready, conv_ready, xs_ready, zh_ready, W_ready,
                  S_ready, y_var, x1_ready, x1_var, modb_ready, gab_ready, ln1_stats, onehot_ready,
                  gate_ready, pos_ready, hid_ready, base_ready, z_ready]
        BY_POOL = [S_decayed, y_power, y_stats, x1_power, x1_stats, ln1_power, ln1_dev, arhs_ready, Bh_ready, xg_ready, h2_scaled, h2_ready, h2g_ready]

        mod_in, consts_in_sb = sem("mod_in"), sem("consts_in_sb")
        win_in, wout_in, ws_in = sem("win_in"), sem("wout_in"), sem("ws_in")
        we_low, we_high = sem("we_low"), sem("we_high")
        cth_done, cs_done, modmm_done, modc_mm, modc_read, mod_set, mod_stored = (sem(n) for n in (
            "cth_done", "cs_done", "modmm_done", "modc_mm", "modc_read", "mod_set", "mod_stored"))
        lnb_done, bmm_done, setup_dve, neg_done, setup_pool, setup_ready = (sem(n) for n in (
            "lnb_done", "bmm_done", "setup_dve", "neg_done", "setup_pool", "setup_ready"))
        pad_ready, pad_stored, tab_ready, tab_dve = (sem(n) for n in (
            "pad_ready", "pad_stored", "tab_ready", "tab_dve"))
        scan_over, power_set, passed = sem("scan_over"), sem("power_set"), sem("passed")

        FIRST = Batch(0, 0)
        PRO2, PRO1 = Turn(Batch(-1, 0), "pro2"), Turn(Batch(-1, 1), "pro1")

        def opened(pe, t, use):
            s = WHERE[use]
            pe.wait_ge(s.free.sem, s.free.at(t.b, s.index(use, t.mode)))
            return s.ap

        def filled(eng, t, use):
            s = WHERE[use]
            eng.wait_ge(s.full.sem, s.full.at(t.b, s.index(use, t.mode) + 1))
            return s.ap

        def rows_left(eng, b):
            eng.wait_ge(scattered, b.i * (2 * 16 * NC) + 16 * (NC * b.par + 1))

        def emptied(eng, t, use):
            s = WHERE[use]
            eng.wait_ge(s.free.sem, s.free.at(t.b, s.index(use, t.mode) + 1))

        def fill(use, ins):
            ins.then_inc(WHERE[use].full.sem, 1)

        def empty(use, ins):
            ins.then_inc(WHERE[use].free.sem, 1)

        def wait(eng, count, b, k):
            eng.wait_ge(count.sem, count.at(b, k))

        def apart(eng):
            eng.sem_inc(passed, 1)

        def turns(eng, body):
            with eng.Fori(0, NB // 2 - 1) as i:
                body(Turn(Batch(i, 0), "full"))
                body(Turn(Batch(i, 1), "full"))
            body(Turn(Batch(NB // 2 - 1, 0), "no_early"))
            body(Turn(Batch(NB // 2 - 1, 1), "last"))


        bx_loaded = [sem("bx_loaded0"), sem("bx_loaded1")]
        rest_loaded = [sem("rest_loaded0"), sem("rest_loaded1")]
        row_out = [sem("row_out0"), sem("row_out1")]
        bturned, gfull, ufull, hturned, dfull = (count(n, 1) for n in (
            "bturned", "gfull", "ufull", "hturned", "dfull"))
        bxT_ready, bth_ready, bhT_ready = (count(n, 1) for n in ("bxT_ready", "bth_ready", "bhT_ready"))
        bhg_ready, bhid_ready, bt_ready, bo_ready = (count(n, 1) for n in (
            "bhg_ready", "bhid_ready", "bt_ready", "bo_ready"))
        Gb, Ub = [banks["W0"], banks["YD"]], [banks["W1"], banks["YO"]]

        def blocks(eng, body, peeled=0):
            pairs = (NBLK - 2) // 2
            for j in range(2 * peeled):
                body(Batch(j // 2, j % 2), 2)
            with eng.Fori(peeled, pairs) as i:
                body(Batch(i, 0), 2)
                body(Batch(i, 1), 2)
            for j in range(2 * pairs, NBLK):
                body(Batch(j // 2, j % 2), min(2, NBLK - 1 - j))

        def table(eng, row, b, most):
            j = b.num()
            return eng.value_load(tabi[0:1, row, bass.ds(j, 1)], min_val=0, max_val=most)

        def landed(eng, sems, b):
            eng.wait_ge(sems[b.par], b.i * 16 + 16)

        def slots_complete(eng):
            eng.wait_ge(tab_ready, 1)
            rows_left(eng, Batch(NB // 2, 0))
            eng.wait_ge(pad_stored, 16 * E)

        def routed_sync(sp):
            slots_complete(sp)

            def load(b):
                first = table(sp, 0, b, E * REG)
                sp.dma_start(bx[b.par], slots[bass.ds(first, P), 0:D]).then_inc(bx_loaded[b.par], 16)

            load(Batch(0, 0))
            load(Batch(0, 1))

            def body(b, ahead):
                if ahead == 2:
                    wait(sp, bturned, b, 1)
                    apart(sp)
                    load(b.plus(2))

            blocks(sp, body)

        def routed_tensor(pe):
            for cnt in (bturned, gfull, ufull, hturned, dfull):
                cnt.start(pe)
            pe.wait_ge(tab_ready, 1)

            def turn_block(b):
                landed(pe, bx_loaded, b)
                wait(pe, bxT_ready, b, -1)
                for k in range(KD):
                    ins = pe.transpose(banks[f"T{b.par}"][:, k * P:(k + 1) * P], bx[b.par][:, k * P:(k + 1) * P], ident)
                ins.then_inc(bturned.sem, 1)

            def gate_up(b):
                at = table(pe, 1, b, (E - 1) * WE)
                wait(pe, bxT_ready, b, 1)
                for ps, done, used_up, first in ((Gb[b.par], gfull, bhg_ready, 0), (Ub[b.par], ufull, bhid_ready, F)):
                    wait(pe, used_up, b, -1)
                    for k in range(KD):
                        ins = pe.matmul(ps[:, :], bxT[b.par][:, k, :], We[:, bass.ds(at + (2 * F * k + first), F)],
                                        start=(k == 0), stop=(k == KD - 1))
                    ins.then_inc(done.sem, 1)

            def turn_hidden(b):
                wait(pe, bhid_ready, b, 1)
                wait(pe, bhT_ready, b, 0)
                for k in range(KF):
                    ins = pe.transpose(banks["SG"][:, k * P:(k + 1) * P], bhid[b.par][:, k * P:(k + 1) * P], ident)
                ins.then_inc(hturned.sem, 1)

            def down(b):
                at = table(pe, 1, b, (E - 1) * WE)
                wait(pe, bhT_ready, b, 1)
                wait(pe, bt_ready, b, 0)
                for k in range(KF):
                    ins = pe.matmul(M[:, 0:D], bhT[b.par][:, k, :],
                                    We[:, bass.ds(at + (KD * 2 * F + D * k), D)], start=(k == 0), stop=(k == KF - 1))
                ins.then_inc(dfull.sem, 1)

            turn_block(Batch(0, 0))
            pe.wait_ge(we_low, 16)
            pe.wait_ge(we_high, 16)
            gate_up(Batch(0, 0))
            turn_block(Batch(0, 1))

            def body(b, ahead):
                turn_hidden(b)
                if ahead >= 1:
                    gate_up(b.plus(1))
                if ahead == 2:
                    turn_block(b.plus(2))
                down(b)

            blocks(pe, body)

        def routed_scalar(act):
            for cnt in (bxT_ready, bth_ready, bhT_ready):
                cnt.start(act)

            def evac_block(b):
                wait(act, bturned, b, 1)
                act.activation(bxT[b.par], banks[f"T{b.par}"][:, 0:KD * P].rearrange("p (k n) -> p k n", k=KD), ACT.Copy)\
                    .then_inc(bxT_ready.sem, 1)

            def tanh_gate(b):
                wait(act, gfull, b, 1)
                wait(act, bhg_ready, b, -1)
                act.activation(bth[b.par], Gb[b.par][:, :], ACT.Tanh, scale=0.5).then_inc(bth_ready.sem, 1)

            def evac_hidden(b):
                wait(act, hturned, b, 1)
                act.activation(bhT[b.par], banks["SG"][:, :].rearrange("p (k n) -> p k n", k=KF), ACT.Copy).then_inc(bhT_ready.sem, 1)

            def before(b):
                return Batch(b.i, 0) if b.par else Batch(b.i - 1, 1)

            def load_rest(b):
                first = table(act, 0, b, E * REG)
                act.dma_start(brest[b.par], slots[bass.ds(first, P), D:ROW]).then_inc(rest_loaded[b.par], 16)

            slots_complete(act)
            load_rest(Batch(0, 0))
            evac_block(Batch(0, 0))
            tanh_gate(Batch(0, 0))
            evac_block(Batch(0, 1))

            def body(b, ahead):
                evac_hidden(b)
                if ahead >= 1:
                    tanh_gate(b.plus(1))
                if ahead == 2:
                    evac_block(b.plus(2))
                if ahead >= 1:
                    if b.par or not isinstance(b.i, int) or b.i > 0:
                        landed(act, row_out, before(b))
                    load_rest(b.plus(1))

            blocks(act, body, 1)

        table_steps = [0]

        def block_table(dve, part):
            def link(ins):
                table_steps[0] += 1
                ins.then_inc(tab_dve, 1)
                dve.wait_ge(tab_dve, table_steps[0])

            wide = lambda a: a.unsqueeze(1).broadcast_to([P, NBLK, E])
            ci = K[:, C_I:C_I + NBLK].unsqueeze(2).broadcast_to([P, NBLK, E])
            co = K[:, C_OFF:C_OFF + NBLK * E].rearrange("p (i e) -> p i e", e=E)
            if part == 0:
                link(dve.tensor_scalar(padf[:, :], carry[:, 0, :], K[:, C_P:C_P + 1], None, ALU.add))
                dve.tensor_copy(padi[:, :], padf[:, :]).then_inc(pad_ready, 1)
                link(dve.tensor_tensor(tab[:, 0, :], carry[:, 0, :], K[:, C_REG:C_REG + E], ALU.subtract))
                link(dve.tensor_tensor(tabj[:, :, :], tab[:, 0, :].unsqueeze(2).broadcast_to([P, E, TOK // P]),
                                       K[:, C_CMP:C_CMP + TOK // P].unsqueeze(1).broadcast_to([P, E, TOK // P]), ALU.is_gt))
                link(dve.tensor_reduce(tab[:, 1, :], tabj[:, :, :], AX.X, ALU.add))
                link(dve.tensor_copy(tab[:, 2, :], tab[:, 1, :]))
            if part == 1:
                for e in range(1, E):
                    link(dve.tensor_tensor(tab[:, 2, e:e + 1], tab[:, 2, e - 1:e], tab[:, 1, e:e + 1], ALU.add))
                link(dve.tensor_tensor(tab[:, 3, :], tab[:, 2, :], tab[:, 1, :], ALU.subtract))
                link(dve.tensor_scalar(tab[:, 4, :], tab[:, 3, :], float(-P), None, ALU.mult))
            if part == 2:
                link(dve.tensor_tensor(tabb[:, 0], ci, wide(tab[:, 2, :]), ALU.is_ge))
                link(dve.tensor_tensor(tabb[:, 1], ci, wide(tab[:, 3, :]), ALU.is_ge))
                link(dve.tensor_tensor(tabb[:, 2], tabb[:, 1], tabb[:, 0], ALU.subtract))
            if part == 3:
                link(dve.tensor_tensor(tabb[:, 0], co, wide(tab[:, 4, :]), ALU.add))
                link(dve.tensor_tensor(tabb[:, 0], tabb[:, 0], tabb[:, 2], ALU.mult))
                link(dve.tensor_reduce(tabr[:, 0, :], tabb[:, 0], AX.X, ALU.add))
                link(dve.tensor_scalar(tabr[:, 0, :], tabr[:, 0, :], float(E * REG), None, ALU.add))
                link(dve.tensor_tensor(tabb[:, 1], tabb[:, 2], wide(K[:, C_E:C_E + E]), ALU.mult))
                link(dve.tensor_reduce(tabr[:, 1, :], tabb[:, 1], AX.X, ALU.add))
                dve.tensor_copy(tabi[:, :, :], tabr[:, :, :]).then_inc(tab_ready, 1)

        def routed_vector(dve):
            for cnt in (bhg_ready, bhid_ready, bt_ready, bo_ready):
                cnt.start(dve)
            def hidden(b):
                q = b.par
                wait(dve, bth_ready, b, 1)
                dve.scalar_tensor_tensor(out=bhg[q], in0=bth[q], scalar=1.0, in1=Gb[q][:, :], op0=ALU.add, op1=ALU.mult)\
                    .then_inc(bhg_ready.sem, 1)
                wait(dve, ufull, b, 1)
                wait(dve, bhg_ready, b, 1)
                dve.tensor_tensor(bhid[q], bhg[q], Ub[q][:, :], ALU.mult).then_inc(bhid_ready.sem, 1)

            def combine(b):
                q = b.par
                wait(dve, dfull, b, 1)
                landed(dve, rest_loaded, b)
                dve.scalar_tensor_tensor(out=bt[q], in0=M[:, 0:D], scalar=0.5, in1=brest[q][:, D:2 * D],
                                         op0=ALU.mult, op1=ALU.mult).then_inc(bt_ready.sem, 1)
                wait(dve, bt_ready, b, 1)
                dve.tensor_tensor(bo[q], bt[q], brest[q][:, 0:D], ALU.add).then_inc(bo_ready.sem, 1)

            hidden(Batch(0, 0))

            def body(b, ahead):
                if ahead >= 1:
                    hidden(b.plus(1))
                combine(b)

            blocks(dve, body)

        def routed_gpsimd(pool):
            slots_complete(pool)

            def body(b, ahead):
                q = b.par
                wait(pool, bo_ready, b, 1)
                apart(pool)
                pool.indirect_dma_start(out=out, out_offset=bass.IndirectOffsetOnAxis(brest[q][:, 2 * D:2 * D + 1].bitcast(I32), 0),
                                        in_=bo[q], in_offset=None, bounds_check=TOK - 1, oob_is_err=False).then_inc(row_out[q], 16)

            blocks(pool, body)
            for q in range(2):
                pool.wait_ge(row_out[q], 16 * ((NBLK + 1 - q) // 2))

        block = ctx.enter_context(nc.Block())
        u_v = u.rearrange("b (c p) d -> b p c d", p=P)

        @block.sync
        def _(sp):
            sp.dma_start(cT[:, :, :], c_t).then_inc(mod_in, 16)
            sp.dma_start(Wmod, w_mod).then_inc(mod_in, 16)
            sp.dma_start(hn[:, :, :], u_v[0]).then_inc(hn_loaded, 16)
            for to, source in ((colp[:, :], cols_in), (K[:, :], consts_in),
                               (rowp[:, :], rows_in.partition_broadcast(P)), (Wr[:, :, :], w_router)):
                sp.dma_start(to, source).then_inc(consts_in_sb, 16)
            sp.dma_start(Win, w_in).then_inc(win_in, 16)
            sp.dma_start(Wout[:, :, :], w_out).then_inc(wout_in, 16)
            for q in range(2):
                sp.dma_start(xin[q][:, :, :], u_v[q]).then_inc(x_loaded[q], 16)
            sp.dma_start(Ws[:, :], w_shared).then_inc(ws_in, 16)
            def load_hn(n, before):
                wait(sp, hT_ready, before, KD)
                apart(sp)
                at = n.num()
                sp.dma_start(hn[:, :, :], u_v[at] if isinstance(at, int) else
                             u_v[bass.ds(at, 1)].rearrange("a p c d -> (a p) c d")).then_inc(hn_loaded, 16)

            def move_ct(n):
                wait(sp, xs_ready, n, 1)
                sp.dma_start(CT[n.par][0:NS, :], BCs[n.par][NS:2 * NS, :]).then_inc(ct_moved[n.par], 16)

            load_hn(Batch(0, 1), FIRST)
            move_ct(FIRST)
            sp.wait_ge(mod_set, 3)
            sp.dma_start(mod_dram, mpre[:, :]).then_inc(mod_stored, 16)
            sp.wait_ge(mod_stored, 16)
            for q in range(2):
                sp.dma_start(mrow[q][:, :, :].rearrange("p m d -> p (m d)"),
                             mod_dram[q].partition_broadcast(P)).then_inc(mod_loaded[q], 16)
            sp.wait_ge(modmm_done, 1)
            sp.dma_start(We[:, 0:(E - LATE) * WE].rearrange("p (e n) -> p e n", n=WE), w_experts[:, 0:E - LATE, :]).then_inc(we_low, 16)
            move_ct(Batch(0, 1))

            def body(t):
                if t.mode == "full":
                    b = t.b
                    load_hn(Batch(b.i + 1, b.par), b.next())
                    wait(sp, x1_ready, b, NC)
                    sp.dma_start(xin[b.par][:, :, :],
                                 u_v[bass.ds(b.num(2), 1)].rearrange("a p c d -> (a p) c d")).then_inc(x_loaded[b.par], 16)
                    move_ct(Batch(b.i + 1, b.par))
                    wait(sp, base_ready, b, NC)
                    apart(sp)
                    wait(sp, gbrow_ready, b, 1)
                    sp.dma_start(mrow[b.par][:, :, :].rearrange("p m d -> p (m d)"),
                                 mod_dram[bass.ds(b.num(2), 1), :].rearrange("a n -> (a n)")
                                 .partition_broadcast(P)).then_inc(mod_loaded[b.par], 16)

            turns(sp, body)
            sp.wait_ge(scan_over, 1)
            sp.dma_start(top.rearrange("p (e n) -> p e n", n=WE), w_experts[:, E - LATE:, :]).then_inc(we_high, 16)
            routed_sync(sp)

        @block.tensor
        def _(pe):
            for s in SLOTS:
                pe.sem_inc(s.full.sem, s.credit())
                pe.sem_inc(s.free.sem, s.credit())

            def project_hT(t):
                wait(pe, hn_ready, t.n, NC)
                for k in range(KD):
                    ps = opened(pe, t, f"EhT{k}")
                    for c in range(NC):
                        ins = pe.transpose(ps[:, c * P:(c + 1) * P], hn[:, c, k * P:(k + 1) * P], ident)
                    fill(f"EhT{k}", ins)

            def project_dt(t):
                ps = opened(pe, t, "Edt")
                for c in range(NC):
                    for k in range(KD):
                        ins = pe.matmul(ps[:, c * H:(c + 1) * H], hT[:, k, c * P:(c + 1) * P],
                                        Win[:, k, NPROJ - H:NPROJ], start=(k == 0), stop=(k == KD - 1))
                fill("Edt", ins)

            def project_x(t, name, first):
                wait(pe, hT_ready, t.n, KD)
                ps = opened(pe, t, name)
                for k in range(KD):
                    ins = pe.matmul(ps, Win[:, k, first:first + P], hT[:, k, :], start=(k == 0), stop=(k == KD - 1))
                fill(name, ins)

            def project_z(t, c):
                ps = opened(pe, t, f"Az{c}")
                for k in range(KD):
                    ins = pe.matmul(ps, hT[:, k, c * P:(c + 1) * P], Win[:, k, 0:DI], start=(k == 0), stop=(k == KD - 1))
                fill(f"Az{c}", ins)

            def turn_B(t):
                wait(pe, xs_ready, t.n, 1)
                ps = opened(pe, t, "AtB")
                apart(pe)
                for c in range(NC):
                    ins = pe.transpose(ps[:, c * NS:(c + 1) * NS], BCs[t.n.par][0:NS, c * P:(c + 1) * P], ident[0:NS, 0:NS])
                fill("AtB", ins)

            def turn_x(t, j):
                wait(pe, xs_ready, t.n, j + 2)
                ps = opened(pe, t, f"AtX{j}")
                for c in range(NC):
                    ins = pe.transpose(ps[:, c * P:(c + 1) * P], xs[j % 2][:, c * P:(c + 1) * P], ident)
                fill(f"AtX{j}", ins)

            def begin_piece(t, k):
                if not t:
                    return
                if k == 0:
                    project_hT(t)
                if k == 1:
                    project_x(t, "ExB", 2 * DI)
                if k == 2:
                    project_dt(t)
                if k in (3, 4):
                    project_x(t, f"Ex{k - 3}", DI + (k - 3) * P)

            def piece(t, k):
                if not t:
                    return
                if k == 0:
                    turn_B(t)
                    turn_x(t, 0)
                if k == 1:
                    project_x(t, "Ax2", DI + 2 * P)
                if k == 2:
                    turn_x(t, 1)
                    project_x(t, "Ax3", DI + 3 * P)
                if k == 3:
                    project_z(t, 0)
                if k == 4:
                    turn_x(t, 2)
                    project_z(t, 1)
                if k == 5:
                    turn_x(t, 3)
                if k >= 6:
                    project_z(t, k - 4)

            def pairs(t, c):
                q = t.b.par
                cs = slice(c * P, (c + 1) * P)
                if c == 0:
                    pe.wait_ge(ct_moved[q], t.b.i * 16 + 16)
                ps = opened(pe, t, f"g{c}")
                fill(f"g{c}", pe.matmul(ps[:, 0:P], BCs[q][0:NS, cs], CT[q][0:NS, cs], start=True, stop=True))

            def scan_1(t, c):
                b = t.b
                q = b.par
                wait(pe, arhs_ready, b, c + 1)
                ps = opened(pe, t, f"seg{c}")
                fill(f"seg{c}", pe.matmul(ps, GT, arhs[c][:, :, :].rearrange("p h l -> p (h l)"), start=True, stop=True))

            def sums(t):
                wait(pe, dt_ready, t.b, 1)
                ps = opened(pe, t, "cu")
                for k, m in enumerate((LE, GT, ONE)):
                    ins = pe.matmul(ps[:, k * NC * H:(k + 1) * NC * H], m, da[t.b.par][:, :, :].rearrange("p c h -> p (c h)"), start=True, stop=True)
                fill("cu", ins)

            def scan_2(t, c):
                b = t.b
                q = b.par
                wait(pe, W_ready, b, c + 1)
                if c == 0:
                    wait(pe, X_ready, b, H)
                ps = opened(pe, t, f"yd{c}")
                for h in range(H):
                    ins = pe.matmul(ps[:, h * HD:(h + 1) * HD], Wm[:, h, :], Xt[q][:, c, h * HD:(h + 1) * HD], start=True, stop=True)
                fill(f"yd{c}", ins)
                if c > 0:
                    wait(pe, S_ready, b, c)
                    ps = opened(pe, t, f"yo{c}")
                    fill(f"yo{c}", pe.matmul(ps, CT[q][0:NS, c * P:(c + 1) * P], St[:, :, :].rearrange("n h p -> n (h p)"), start=True, stop=True))
                if c < NC - 1:
                    wait(pe, Bh_ready, b, c + 1)
                    ps = opened(pe, t, f"dS{c}")
                    for h in range(H):
                        ins = pe.matmul(ps[0:NS, h * HD:(h + 1) * HD], Bh[:, h, :], Xt[q][:, c, h * HD:(h + 1) * HD], start=True, stop=True)
                    fill(f"dS{c}", ins)

            def turn_y(t, c):
                wait(pe, yn_ready, t.b, c + 1)
                ps = opened(pe, t, f"yT{c}")
                for k in range(KI):
                    ins = pe.transpose(ps[:, k * P:(k + 1) * P], yn[c % 2][:, k * P:(k + 1) * P], ident)
                fill(f"yT{c}", ins)

            def project_y(t, c):
                wait(pe, yT_ready, t.b, c + 1)
                ps = opened(pe, t, f"op{c}")
                for k in range(KI):
                    ins = pe.matmul(ps[:, 0:D], yT[:, k, :], Wout[:, k, :], start=(k == 0), stop=(k == KI - 1))
                fill(f"op{c}", ins)

            def turn_h2(t, c):
                wait(pe, h2_ready, t.b, c + 1)
                ps = opened(pe, t, f"h2T{c}")
                for k in range(KD):
                    ins = pe.transpose(ps[:, k * P:(k + 1) * P], h2[:, c, k * P:(k + 1) * P], ident)
                fill(f"h2T{c}", ins)

            def gate_up(t, j):
                for name, first in ((f"Cg{j}", j * P), (f"Cu{j}", F + j * P)):
                    ps = opened(pe, t, name)
                    for k in range(KD):
                        ins = pe.matmul(ps, Wsg[:, k, first:first + P], h2T[:, k, :], start=(k == 0), stop=(k == KD - 1))
                    fill(name, ins)

            def route(t, c):
                wait(pe, h2T_ready, t.b, c + 1)
                ps = opened(pe, t, "rt") if c == 0 else WHERE["rt"].ap
                for k in range(KD):
                    ins = pe.matmul(ps[:, c * E:(c + 1) * E], h2T[:, k, c * P:(c + 1) * P], Wr[:, k, :], start=(k == 0), stop=(k == KD - 1))
                if c == NC - 1:
                    fill("rt", ins)

            def mlp(t, m):
                b = t.b
                gate_up(t, 0)
                begin_piece(m, 2)
                gate_up(t, 1)
                wait(pe, onehot_ready, b, 1)
                ps = opened(pe, t, "rk")
                oh = onehot[:, :, :].rearrange("p c e -> p (c e)")
                pe.matmul(ps[:, 0:NC * E], LT, oh, start=True, stop=True)
                fill("rk", pe.matmul(ps[:, NC * E:2 * NC * E], ONE, oh, start=True, stop=True))
                gate_up(t, 2)
                begin_piece(m, 3)
                gate_up(t, 3)
                begin_piece(m, 4)
                wait(pe, hid_ready, b, KF)
                for c in range(NC):
                    ps = opened(pe, t, f"dn{c}")
                    for j in range(KF):
                        ins = pe.matmul(ps[:, 0:D], hid[:, j, c * P:(c + 1) * P], Wsd[:, j, :], start=(j == 0), stop=(j == KF - 1))
                    fill(f"dn{c}", ins)

            def body(t):
                n, m = t.projecting(1), t.projecting(2)
                sums(t)
                pairs(t, 0)
                scan_1(t, 0)
                pairs(t, 1)
                for s in range(NC):
                    if s < NC - 1:
                        scan_1(t, s + 1)
                    scan_2(t, s)
                    if s > 0:
                        turn_y(t, s - 1)
                    piece(n, (0, 2, 4, 5)[s])
                    if s > 0:
                        project_y(t, s - 1)
                    if s + 2 < NC:
                        pairs(t, s + 2)
                    if s < 2:
                        piece(n, (1, 3)[s])
                    if s == NC - 1:
                        piece(n, 6)
                    if s > 1:
                        turn_h2(t, s - 2)
                turn_y(t, NC - 1)
                project_y(t, NC - 1)
                turn_h2(t, NC - 2)
                piece(n, 7)
                for c in range(NC - 1):
                    route(t, c)
                begin_piece(m, 0)
                turn_h2(t, NC - 1)
                begin_piece(m, 1)
                route(t, NC - 1)
                mlp(t, m)

            pe.wait_ge(mod_in, 32)
            pe.wait_ge(cs_done, 2)
            for j in range(4):
                for k in range(KD):
                    ins = pe.matmul(M[:, j * NB:(j + 1) * NB], Wmod[:, k, j * P:(j + 1) * P], cTs[:, k, :], start=(k == 0), stop=(k == KD - 1))
            ins.then_inc(modc_mm, 1)
            for j, n in enumerate(("YO", "SG")):
                for k in range(KD):
                    ins = pe.matmul(banks[n][0:NB, :], cTs[:, k, :], Wmod[:, k, (j + 1) * 512:(j + 2) * 512], start=(k == 0), stop=(k == KD - 1))
            ins.then_inc(modmm_done, 1)
            pe.wait_ge(consts_in_sb, 64)
            begin_piece(PRO2.projecting(2), 0)
            pe.wait_ge(lnb_done, 1)
            pe.wait_ge(wout_in, 16)
            for k in range(KI):
                ins = pe.matmul(banks["YD"][:, 0:D], lnb_b[:, k, :], Wout[:, k, :], start=(k == 0), stop=(k == KI - 1))
            ins.then_inc(bmm_done, 1)
            pe.wait_ge(win_in, 16)
            pe.wait_ge(modc_read, 1)
            for k in range(1, 5):
                begin_piece(PRO2.projecting(2), k)
            for k in range(8):
                piece(PRO1.projecting(1), k)
            for k in range(5):
                begin_piece(PRO1.projecting(2), k)
            pe.wait_ge(setup_ready, 1)
            pe.wait_ge(ws_in, 16)
            turns(pe, body)
            routed_tensor(pe)

        @block.scalar
        def _(act):
            for cnt in BY_ACT:
                cnt.start(act)

            def evac_hT(t):
                wait(act, modb_ready, t.n, 1)
                for k in range(KD):
                    ps = filled(act, t, f"EhT{k}")
                    ins = act.activation(hT[:, k, :], ps, ACT.Identity, bias=modb[:, k:k + 1], scale=modb[:, 2 + k:3 + k])
                    empty(f"EhT{k}", ins)
                for k in range(KD):
                    emptied(act, t, f"EhT{k}")
                    act.sem_inc(hT_ready.sem, 1)

            def evac_x(t, q):
                name = ("ExB", "Ex0", "Ex1", "Ax2", "Ax3")[q]
                j = (q - 1) % NT
                n = t.n
                ps = filled(act, t, name)
                wait(act, conv_ready, n, max(q - 1, 0))
                act.activation(xpre[q % 2][:, 3:], ps, ACT.Identity, bias=colp[:, IB + j:IB + j + 1]).then_inc(xpre_ready.sem, 1)
                wait(act, xpre_ready, n, q + 1)
                act.sem_inc(WHERE[name].free.sem, 1)
                wait(act, xs_ready, n, max(q - 1, 0))
                act.activation(cacc[q % 2][:, :], xpre[q % 2][:, 0:SEQ], ACT.Identity, bias=colp[:, CB + j:CB + j + 1],
                               scale=colp[:, CW + 4 * j:CW + 4 * j + 1]).then_inc(tap_ready.sem, 1)

            def tanh_x(t, q):
                wait(act, conv_ready, t.n, q + 1)
                act.activation(ctanh[q % 2][:, :], cacc[q % 2][:, :], ACT.Tanh).then_inc(th_ready.sem, 1)

            def evac_X(t, j):
                n = t.n
                ps = filled(act, t, f"AtX{j}")
                wait(act, dt_ready, n, 1)
                for c in range(NC):
                    ins = act.activation(Xt[n.par][:, c, j * P:(j + 1) * P], ps[:, c * P:(c + 1) * P], ACT.Copy,
                                         scale=dt[n.par][:, c, j:j + 1])
                ins.then_inc(X_ready.sem, 1)
                wait(act, X_ready, n, j + 1)
                act.sem_inc(WHERE[f"AtX{j}"].free.sem, 1)

            def tanh_z(t, c):
                wait(act, zh_ready, t.n, c + 1)
                wait(act, z_ready, t.n, c - 1)
                act.activation(zth[c % 2][:, :], zh[c % 2][:, :], ACT.Tanh).then_inc(zth_ready.sem, 1)

            def norm_hn(n):
                wait(act, ln1_dev, n, 1)
                for c in range(NC):
                    act.activation(hn[:, c, :], hn[:, c, :], ACT.Identity, bias=nb1[:, c:c + 1], scale=rs1[:, c:c + 1])\
                        .then_inc(hn_ready.sem, 1)

            def begin_piece(t, k):
                if not t:
                    return
                if k == 0:
                    evac_hT(t)
                if k == 1:
                    evac_x(t, 0)
                if k == 2:
                    tanh_x(t, 0)
                    wait(act, dtx_ready, t.n, 1)
                    act.activation(dts[:, 2, :], dts[:, 1, :], ACT.Exp, scale=-1.0).then_inc(dte_ready.sem, 1)
                if k == 3:
                    evac_x(t, 1)
                if k == 4:
                    tanh_x(t, 1)
                    evac_x(t, 2)
                if k == 5:
                    tanh_x(t, 2)

            def piece(t, k):
                if not t:
                    return
                if k == 0:
                    ps = filled(act, t, "AtB")
                    empty("AtB", act.activation(Btok[t.n.par][:, :, :].rearrange("p c n -> p (c n)"), ps[:, 0:NC * NS], ACT.Copy))
                    emptied(act, t, "AtB")
                    act.sem_inc(btok_ready.sem, 1)
                    evac_X(t, 0)
                if k == 1:
                    evac_x(t, 3)
                if k == 2:
                    evac_X(t, 1)
                    evac_x(t, 4)
                    tanh_x(t, 3)
                if k == 3:
                    tanh_x(t, 4)
                if k == 4:
                    evac_X(t, 2)
                    tanh_z(t, 0)
                if k == 5:
                    evac_X(t, 3)
                    tanh_z(t, 1)
                if k >= 6:
                    tanh_z(t, k - 4)

            def exps(t, c):
                b = t.b
                ps = filled(act, t, f"seg{c}")
                wait(act, W_ready, b, c - 1)
                act.activation(Ex[c % 2][:, :, :].rearrange("p h l -> p (h l)"), ps, ACT.Exp).then_inc(E_ready.sem, 1)
                wait(act, E_ready, b, c + 1)
                act.sem_inc(SG.free.sem, 1)

            def carried(t, c):
                b = t.b
                yo = filled(act, t, f"yo{c}")
                wait(act, yn_ready, b, c - 1)
                for h in range(H):
                    ins = act.activation(y[c % 2][:, h * HD:(h + 1) * HD], yo[:, h * HD:(h + 1) * HD], ACT.Copy, scale=ec[:, 0, c, h:h + 1])
                ins.then_inc(yo_ready.sem, 1)
                wait(act, yo_ready, b, c)
                act.sem_inc(YO.free.sem, 1)

            def norm_y(t, c):
                wait(act, y_stats, t.b, c + 1)
                act.activation(yn[c % 2][:, :], y[c % 2][:, :], ACT.Identity, bias=rs[c % 2][:, 1:2], scale=rs[c % 2][:, 0:1]).then_inc(yn_ready.sem, 1)

            def evac_yT(t, c):
                ps = filled(act, t, f"yT{c}")
                act.activation(yT[:, :, :].rearrange("p k n -> p (k n)"), ps, ACT.Copy).then_inc(yT_ready.sem, 1)
                wait(act, yT_ready, t.b, c + 1)
                act.sem_inc(WHERE[f"yT{c}"].free.sem, 1)

            def norm_x1(t, c):
                wait(act, x1_stats, t.b, c + 1)
                wait(act, h2_ready, t.b, c - 1)
                act.activation(n2[c % 2][:, :], rowbuf[:, c, D:2 * D], ACT.Identity, bias=rs2[c % 2][:, 1:2], scale=rs2[c % 2][:, 0:1]).then_inc(n2_ready.sem, 1)

            def evac_h2T(t, c):
                ps = filled(act, t, f"h2T{c}")
                act.activation(h2T[:, :, c * P:(c + 1) * P], ps[:, 0:KD * P].rearrange("p (k n) -> p k n", k=KD), ACT.Copy).then_inc(h2T_ready.sem, 1)
                wait(act, h2T_ready, t.b, c + 1)
                act.sem_inc(WHERE[f"h2T{c}"].free.sem, 1)

            def body(t):
                b = t.b
                n, m = t.projecting(1), t.projecting(2)
                ps = filled(act, t, "cu")
                act.activation(ec[:, :, :, :].rearrange("p k c h -> p (k c h)"), ps[:, 0:3 * NC * H], ACT.Exp).then_inc(ec_ready.sem, 1)
                wait(act, ec_ready, b, 1)
                act.sem_inc(WHERE["cu"].free.sem, 1)
                exps(t, 0)
                for s in range(NC):
                    if s < NC - 1:
                        exps(t, s + 1)
                    if s > 0:
                        carried(t, s)
                        evac_yT(t, s - 1)
                    if s > 1:
                        norm_x1(t, s - 2)
                    piece(n, (0, 2, 4, 5)[s])
                    norm_y(t, s)
                    if s < 2:
                        piece(n, (1, 3)[s])
                    else:
                        evac_h2T(t, s - 2)
                evac_yT(t, NC - 1)
                norm_x1(t, NC - 2)
                piece(n, 6)
                evac_h2T(t, NC - 2)
                if m:
                    norm_hn(m.n)
                norm_x1(t, NC - 1)
                begin_piece(m, 0)
                piece(n, 7)
                evac_h2T(t, NC - 1)
                begin_piece(m, 1)
                wait(act, onehot_ready, b, 1)
                act.activation(mx[:, 1, :], mx[:, 0, :], ACT.Tanh, scale=0.5).then_inc(gth_ready.sem, 1)

                def tanh_gate(j):
                    ps = filled(act, t, f"Cg{j}")
                    wait(act, hid_ready, b, j - 1)
                    act.activation(th[j % 2][:, :], ps, ACT.Tanh, scale=0.5).then_inc(fth_ready.sem, 1)

                tanh_gate(0)
                begin_piece(m, 2)
                rows_left(act, b)
                act.wait_ge(mod_loaded[b.par], b.i * 16 + 16)
                for c in range(NC):
                    ins = act.activation(rowbuf[:, c, 2 * D:3 * D], mrow[b.par][:, 3, :], ACT.Copy)
                ins.then_inc(gbrow_ready.sem, 1)
                for j in range(1, KF):
                    tanh_gate(j)
                    if j > 1:
                        begin_piece(m, j + 1)
                begin_piece(m, 5)

            act.wait_ge(mod_in, 32)
            act.activation(cth[:, :, :], cT[:, :, :], ACT.Tanh, scale=0.5).then_inc(cth_done, 1)
            act.wait_ge(consts_in_sb, 64)
            act.activation(negA[:, :], rowp[:, AL:AL + H], ACT.Exp).then_inc(neg_done, 1)
            norm_hn(FIRST)
            for k in range(6):
                begin_piece(PRO2.projecting(2), k)
            for k in range(8):
                if k == 3:
                    norm_hn(Batch(0, 1))
                if k == 7:
                    begin_piece(PRO1.projecting(2), 0)
                piece(PRO1.projecting(1), k)
            for k in range(1, 6):
                begin_piece(PRO1.projecting(2), k)
            turns(act, body)
            routed_scalar(act)

        @block.vector
        def _(dve):
            for cnt in BY_DVE:
                cnt.start(dve)
            ca, cb_, cl = Chain(dve, dve_a), Chain(dve, dve_b), Chain(dve, dve_l)

            def ln1(b):
                cl.begin(b)
                dve.wait_ge(hn_loaded, b.i * 32 + (16 * b.par + 16))
                for c in range(NC):
                    ins = dve.bn_stats(st1[:, c, :], hn[:, c, :])
                cl.link(ins, apart)
                for c in range(NC):
                    ins = dve.bn_aggr(mv1[:, c, :], st1[:, c, :])
                cl.link(ins)
                dve.tensor_scalar(nm1[:, :], mv1[:, :, 0], -1.0, None, ALU.mult)
                dve.tensor_scalar(vl1[:, :], mv1[:, :, 1], EPS, None, ALU.add).then_inc(ln1_stats.sem, 1)
                cl.end()

            def dt_1(t):
                n = t.n
                ps = filled(dve, t, "Edt")
                v = dts[:, 0, :].rearrange("p (c h) -> p c h", c=NC)
                empty("Edt", dve.tensor_tensor(v, ps[:, 0:NC * H].rearrange("p (c h) -> p c h", c=NC),
                                               dtb[:, :].unsqueeze(1).broadcast_to([P, NC, H]), ALU.add))
                emptied(dve, t, "Edt")
                dve.scalar_tensor_tensor(out=dts[:, 1, :], in0=dts[:, 0, :], scalar=-1.0, in1=dts[:, 0, :],
                                         op0=ALU.mult, op1=ALU.max).then_inc(dtx_ready.sem, 1)

            def dt_2(t):
                n = t.n
                wait(dve, dte_ready, n, 1)
                d = [dts[:, k, :] for k in range(8)]
                ca.link(dve.tensor_scalar(d[3], d[2], 2.0, None, ALU.add))
                ca.link(dve.reciprocal(d[4], d[3]))
                ca.link(dve.tensor_tensor(d[5], d[2], d[4], ALU.mult))
                ca.link(dve.tensor_tensor(d[6], d[5], d[5], ALU.mult))
                ca.link(dve.tensor_scalar(d[7], d[6], 1.0 / (2 * LOG_TERMS - 1), None, ALU.mult))
                for k in range(LOG_TERMS - 2, 0, -1):
                    ca.link(dve.scalar_tensor_tensor(out=d[7], in0=d[7], scalar=1.0 / (2 * k + 1), in1=d[6], op0=ALU.add, op1=ALU.mult))
                ca.link(dve.scalar_tensor_tensor(out=d[7], in0=d[7], scalar=1.0, in1=d[5], op0=ALU.add, op1=ALU.mult))
                ca.link(dve.tensor_scalar(d[3], d[0], 0.0, None, ALU.max))
                v = lambda a: a.rearrange("p (c h) -> p c h", c=NC)
                ca.link(dve.scalar_tensor_tensor(out=dt[n.par][:, :, :], in0=v(d[7]), scalar=2.0, in1=v(d[3]), op0=ALU.mult, op1=ALU.add))
                dve.tensor_tensor(da[n.par][:, :, :], dt[n.par][:, :, :], negA[:, :].unsqueeze(1).broadcast_to([P, NC, H]),
                                  ALU.mult).then_inc(dt_ready.sem, 1)

            def conv(t, q):
                j = (q - 1) % NT
                wait(dve, tap_ready, t.n, q + 1)
                for k in (1, 2, 3):
                    ins = dve.scalar_tensor_tensor(out=cacc[q % 2][:, :], in0=xpre[q % 2][:, k:k + SEQ],
                                                   scalar=colp[:, CW + 4 * j + k:CW + 4 * j + k + 1], in1=cacc[q % 2][:, :],
                                                   op0=ALU.mult, op1=ALU.add)
                    if k < 3:
                        ca.link(ins)
                ins.then_inc(conv_ready.sem, 1)

            def finish_x(t, q):
                n = t.n
                wait(dve, th_ready, n, q + 1)
                if q == 0:
                    o = BCs[n.par][:, :]
                else:
                    o = xs[(q - 1) % 2][:, :]
                    wait(dve, X_ready, n, max(q - 2, 0))
                dve.scalar_tensor_tensor(out=o, in0=ctanh[q % 2][:, :], scalar=1.0, in1=cacc[q % 2][:, :],
                                         op0=ALU.add, op1=ALU.mult).then_inc(xs_ready.sem, 1)

            def half_z(t, c):
                n = t.n
                ps = filled(dve, t, f"Az{c}")
                wait(dve, z_ready, n, c - 1)
                dve.scalar_tensor_tensor(out=zh[c % 2][:, :], in0=ps, scalar=0.5, in1=rowp[:, ZB:ZB + DI],
                                         op0=ALU.mult, op1=ALU.add).then_inc(zh_ready.sem, 1)
                wait(dve, zh_ready, n, c + 1)
                dve.sem_inc(WHERE[f"Az{c}"].free.sem, 1)

            def begin_piece(t, k):
                if not t:
                    return
                if k == 0:
                    ca.begin(t.n)
                    wait(dve, hT_ready, t.n, 0)
                    at = t.n.num()
                    dve.tensor_copy(modb[:, :], modc[:, :, at] if isinstance(at, int) else
                                    modc[:, :, bass.ds(at, 1)].rearrange("p m a -> p (m a)")).then_inc(modb_ready.sem, 1)
                if k == 1:
                    conv(t, 0)
                if k == 2:
                    dt_1(t)
                    finish_x(t, 0)
                    dt_2(t)
                if k == 3:
                    conv(t, 1)
                if k == 4:
                    finish_x(t, 1)
                if k == 5:
                    conv(t, 2)
                if k == 6:
                    finish_x(t, 2)
                    ca.end(6 + LOG_TERMS + 2 * EARLY_X)

            def piece(t, k):
                if not t:
                    return
                if k == 0:
                    ca.begin(t.n, 6 + LOG_TERMS + 2 * EARLY_X)
                if k == 1:
                    conv(t, 3)
                if k == 2:
                    finish_x(t, 3)
                    conv(t, 4)
                    ca.end()
                if k == 3:
                    finish_x(t, 4)
                    half_z(t, 0)
                if k == 4:
                    half_z(t, 1)
                if k == 5:
                    finish_z(t, 0)
                if k == 6:
                    finish_z(t, 1)
                    half_z(t, 2)
                if k == 7:
                    half_z(t, 3)
                    finish_z(t, 2)
                if k == 8:
                    finish_z(t, 3)

            def finish_z(t, c):
                n = t.n
                wait(dve, zth_ready, n, c + 1)
                dve.scalar_tensor_tensor(out=Zs[n.par][:, c, :], in0=zth[c % 2][:, :], scalar=1.0, in1=zh[c % 2][:, :],
                                         op0=ALU.add, op1=ALU.mult).then_inc(z_ready.sem, 1)

            def mask_g(t, c):
                ps = filled(dve, t, f"g{c}")
                wait(dve, W_ready, t.b, c)
                empty(f"g{c}", dve.tensor_tensor(Gm[:, :], ps[:, 0:P], LE, ALU.mult))
                emptied(dve, t, f"g{c}")

            def mask_w(t, c):
                b = t.b
                wait(dve, E_ready, b, c + 1)
                dve.tensor_tensor(Wm[:, :, :], Ex[c % 2][:, :, :], Gm[:, :].unsqueeze(1).broadcast_to([P, H, P]), ALU.mult)\
                    .then_inc(W_ready.sem, 1)

            def combine(t, c):
                b = t.b
                q = c % 2
                yd = filled(dve, t, f"yd{c}")
                wait(dve, z_ready, b, c + 1)
                wait(dve, yn_ready, b, c - 1)
                if c > 0:
                    wait(dve, yo_ready, b, c)
                    dve.tensor_tensor(y[q][:, :], y[q][:, :], yd, ALU.add).then_inc(YD.free.sem, 1)
                    emptied(dve, t, f"yd{c}")
                    cb_.link(dve.tensor_tensor(y[q][:, :], y[q][:, :], Zs[b.par][:, c, :], ALU.mult))
                else:
                    dve.tensor_tensor(y[q][:, :], yd, Zs[b.par][:, c, :], ALU.mult).then_inc(YD.free.sem, 1)
                    emptied(dve, t, f"yd{c}")
                cb_.link(dve.bn_stats(st[:, :], y[q][:, :]), apart)
                cb_.link(dve.bn_aggr(mvy[q][:, 0:2], st[:, :]))
                dve.tensor_scalar(mvy[q][:, 2:3], mvy[q][:, 1:2], EPS, None, ALU.add).then_inc(y_var.sem, 1)

            def state(t, c):
                b = t.b
                flat = St[:, :, :].rearrange("n h p -> n (h p)")
                if c > 0:
                    wait(dve, S_decayed, b, c)
                ps = filled(dve, t, f"dS{c}")
                if c == 0:
                    dve.tensor_copy(flat, ps[0:NS, :]).then_inc(S_ready.sem, 1)
                else:
                    dve.tensor_tensor(flat, flat, ps[0:NS, :], ALU.add).then_inc(S_ready.sem, 1)
                wait(dve, S_ready, b, c + 1)
                dve.sem_inc(SG.free.sem, 1)

            def residual(t, c):
                b = t.b
                q = c % 2
                x1 = rowbuf[:, c, D:2 * D]
                if c == 0:
                    wait(dve, xg_ready, b, 1)
                    rows_left(dve, b)
                ps = filled(dve, t, f"op{c}")
                empty(f"op{c}", dve.tensor_tensor(t1[:, :], ps[:, 0:D], mrow[b.par][:, 0, :], ALU.mult))
                emptied(dve, t, f"op{c}")
                dve.tensor_tensor(x1, t1[:, :], xin[b.par][:, c, :], ALU.add).then_inc(x1_ready.sem, 1)
                wait(dve, x1_ready, b, c + 1)
                wait(dve, n2_ready, b, c - 1)
                cb_.link(dve.bn_stats(st[:, :], x1), apart)
                cb_.link(dve.bn_aggr(mvx[q][:, 0:2], st[:, :]))
                dve.tensor_scalar(mvx[q][:, 2:3], mvx[q][:, 1:2], EPS, None, ALU.add).then_inc(x1_var.sem, 1)

            def route(t):
                b = t.b
                ps = filled(dve, t, "rt")
                empty("rt", dve.tensor_copy(lg[:, :, :].rearrange("p c e -> p (c e)"), ps[:, 0:NC * E]))
                emptied(dve, t, "rt")
                cb_.link(dve.tensor_reduce(mx[:, 0, :], lg[:, :, :], AX.X, ALU.max))
                cb_.link(dve.tensor_tensor(rt[:, 0], lg[:, :, :], mx[:, 0, :].unsqueeze(2).broadcast_to([P, NC, E]), ALU.is_equal))
                cb_.link(dve.tensor_tensor(rt[:, 1], rt[:, 0], K[:, C_TIE:C_TIE + E].unsqueeze(1).broadcast_to([P, NC, E]), ALU.mult))
                cb_.link(dve.tensor_reduce(mx[:, 2, :], rt[:, 1], AX.X, ALU.max))
                dve.tensor_tensor(onehot[:, :, :], rt[:, 1], mx[:, 2, :].unsqueeze(2).broadcast_to([P, NC, E]), ALU.is_equal)\
                    .then_inc(onehot_ready.sem, 1)

            def place(t):
                b = t.b
                wait(dve, gth_ready, b, 1)
                dve.tensor_scalar(mx[:, 3, :], mx[:, 1, :], 0.5, 0.5, ALU.mult, ALU.add).then_inc(gate_ready.sem, 1)
                ps = filled(dve, t, "rk")
                for c in range(NC):
                    cb_.link(dve.tensor_tensor(carry[:, c + 1, :], carry[:, c, :], ps[:, (NC + c) * E:(NC + c + 1) * E], ALU.add))
                empty("rk", dve.tensor_tensor(rt[:, 2], carry[:, 0:NC, :],
                                              ps[:, 0:NC * E].rearrange("p (c e) -> p c e", c=NC), ALU.add))
                emptied(dve, t, "rk")
                cb_.link(dve.tensor_copy(carry[:, 0, :], carry[:, NC, :]))
                cb_.link(dve.tensor_tensor(rt[:, 3], rt[:, 2], onehot[:, :, :], ALU.mult))
                cb_.link(dve.tensor_reduce(posf[:, :], rt[:, 3], AX.X, ALU.add))
                cb_.link(dve.tensor_copy(posi[:, :], posf[:, :]))
                dve.tensor_copy(rowbuf[:, :, 3 * D].bitcast(I32), tidf[:, :]).then_inc(pos_ready.sem, 1)
                wait(dve, pos_ready, b, 1)
                cb_.link(dve.tensor_scalar(tidf[:, :], tidf[:, :], float(SEQ), None, ALU.add))

            def hidden(t, j):
                b = t.b
                wait(dve, fth_ready, b, j + 1)
                g, up = WHERE[f"Cg{j}"], WHERE[f"Cu{j}"]
                empty(f"Cg{j}", dve.scalar_tensor_tensor(out=acc[j % 2][:, :], in0=th[j % 2][:, :], scalar=1.0, in1=g.ap,
                                                         op0=ALU.add, op1=ALU.mult))
                emptied(dve, t, f"Cg{j}")
                filled(dve, t, f"Cu{j}")
                dve.tensor_tensor(hid[:, j, :], acc[j % 2][:, :], up.ap, ALU.mult).then_inc(hid_ready.sem, 1)
                wait(dve, hid_ready, b, j + 1)
                dve.sem_inc(up.free.sem, 1)

            def base(t, c):
                b = t.b
                ps = filled(dve, t, f"dn{c}")
                empty(f"dn{c}", dve.scalar_tensor_tensor(out=t1[:, :], in0=ps[:, 0:D], scalar=0.5, in1=mrow[b.par][:, 3, :],
                                                         op0=ALU.mult, op1=ALU.mult))
                emptied(dve, t, f"dn{c}")
                dve.tensor_tensor(rowbuf[:, c, D:2 * D], rowbuf[:, c, D:2 * D], t1[:, :], ALU.add).then_inc(base_ready.sem, 1)
                wait(dve, base_ready, b, c + 1)

            def body(t):
                b = t.b
                n, m = t.projecting(1), t.projecting(2)
                cb_.begin(b)
                dve.wait_ge(mod_loaded[b.par], b.i * 16 + 16)
                dve.tensor_tensor(gab[:, :], mrow[b.par][:, 0, :], brow[:, :], ALU.mult).then_inc(gab_ready.sem, 1)
                mask_g(t, 0)
                mask_w(t, 0)
                mask_g(t, 1)
                for s in range(NC):
                    combine(t, s)
                    if s < NC - 1:
                        mask_w(t, s + 1)
                        state(t, s)
                    elif t.mode == "last":
                        dve.sem_inc(scan_over, 1)
                    if s + 2 < NC:
                        mask_g(t, s + 2)
                    piece(n, (0, 2, 4, 5)[s])
                    if s > 0:
                        residual(t, s - 1)
                    if s < 2:
                        piece(n, (1, 3)[s])
                if m:
                    ln1(m.n)
                begin_piece(m, 0)
                piece(n, 6)
                residual(t, NC - 1)
                piece(n, 7)
                route(t)
                begin_piece(m, 1)
                piece(n, 8)
                def table(part):
                    if t.mode == "last":
                        block_table(dve, part)

                hidden(t, 0)
                begin_piece(m, 2)
                hidden(t, 1)
                if t.mode != "last":
                    hidden(t, 2)
                place(t)
                table(0)
                if t.mode == "last":
                    hidden(t, 2)
                begin_piece(m, 3)
                table(1)
                hidden(t, 3)
                begin_piece(m, 4)
                table(2)
                base(t, 0)
                begin_piece(m, 5)
                base(t, 1)
                base(t, 2)
                begin_piece(m, 6)
                base(t, 3)
                table(3)
                cb_.end()

            steps = [0]

            def link(ins):
                steps[0] += 1
                ins.then_inc(setup_dve, 1)
                dve.wait_ge(setup_dve, steps[0])

            dve.wait_ge(mod_in, 32)
            dve.wait_ge(cth_done, 1)
            dve.scalar_tensor_tensor(out=cTs[:, :, :], in0=cth[:, :, :], scalar=1.0, in1=cT[:, :, :], op0=ALU.add, op1=ALU.mult).then_inc(cs_done, 1)
            dve.wait_ge(cs_done, 1)
            dve.tensor_scalar(cTs[:, :, :], cTs[:, :, :], 0.5, None, ALU.mult).then_inc(cs_done, 1)
            ln1(FIRST)
            dve.wait_ge(consts_in_sb, 64)
            for k in range(KI):
                ins = dve.tensor_scalar(lnb_b[:, k, :], ONE, colp[:, LB + k:LB + k + 1], None, ALU.mult)
            ins.then_inc(lnb_done, 1)
            link(dve.tensor_scalar(colp[:, CW:CW + 4 * NT + NT], colp[:, CW:CW + 4 * NT + NT], 0.5, None, ALU.mult))
            link(dve.tensor_scalar(rowp[:, ZB:ZB + DI], rowp[:, ZB:ZB + DI], 0.5, None, ALU.mult))
            link(dve.tensor_tensor(dtb[:, :], rowp[:, DTB:DTB + H], rowp[:, DTB2:DTB2 + H], ALU.add))
            dve.wait_ge(neg_done, 1)
            link(dve.tensor_scalar(negA[:, :], negA[:, :], -1.0, None, ALU.mult))
            link(dve.tensor_copy(carry[:, 0, :], K[:, C_REG:C_REG + E]))
            link(dve.tensor_copy(tidf[:, :], K[:, C_TID:C_TID + NC]))
            for q in range(2):
                ins = dve.memset(xpre[q][:, 0:3], 0.0)
            link(ins)
            dve.wait_ge(modc_mm, 1)
            link(dve.tensor_copy(modc[:, 0:2, :].rearrange("p m b -> p (m b)"), M[:, 0:2 * NB]))
            link(dve.tensor_scalar(modc[:, 2:4, :].rearrange("p m b -> p (m b)"), M[:, 2 * NB:4 * NB], 1.0, None, ALU.add))
            dve.sem_inc(modc_read, 1)
            begin_piece(PRO2.projecting(2), 0)
            dve.wait_ge(modmm_done, 1)
            ga, sb_, cbm, gb = banks["YO"][0:NB, 0:D], banks["YO"][0:NB, D:2 * D], banks["SG"][0:NB, 0:D], banks["SG"][0:NB, D:2 * D]
            for k, g in enumerate((ga, gb)):
                m = mabs[:, k * D:(k + 1) * D]
                link(dve.tensor_scalar(m, g, -1.0, None, ALU.mult))
                link(dve.scalar_tensor_tensor(out=m, in0=m, scalar=0.25, in1=g, op0=ALU.max, op1=ALU.max))
                link(dve.tensor_scalar(msgn[:, k * D:(k + 1) * D], g, 0.0, 2.0, ALU.is_ge, ALU.mult))
                dve.scalar_tensor_tensor(out=mpre[:, 3 * k * D:(3 * k + 1) * D], in0=msgn[:, k * D:(k + 1) * D], scalar=-1.0,
                                         in1=mabs[:, k * D:(k + 1) * D], op0=ALU.add, op1=ALU.mult).then_inc(mod_set, 1)
            link(dve.tensor_scalar(mpre[:, D:2 * D], cbm, 1.0, None, ALU.add))
            dve.tensor_copy(mpre[:, 2 * D:3 * D], sb_).then_inc(mod_set, 1)
            dve.wait_ge(bmm_done, 1)
            link(dve.tensor_tensor(brow[:, :], banks["YD"][:, 0:D], rowp[:, OB:OB + D], ALU.add))
            for k in range(KI):
                ins = dve.tensor_scalar(Wout[:, k, :], Wout[:, k, :], colp[:, LW + k:LW + k + 1], None, ALU.mult)
            link(ins)
            dve.wait_ge(mod_set, 3)
            dve.sem_inc(setup_ready, 1)
            for k in range(1, 7):
                begin_piece(PRO2.projecting(2), k)
            for k in range(9):
                if k == 1:
                    ln1(Batch(0, 1))
                if k == 6:
                    begin_piece(PRO1.projecting(2), 0)
                piece(PRO1.projecting(1), k)
            for k in range(1, 7):
                begin_piece(PRO1.projecting(2), k)
            turns(dve, body)
            routed_vector(dve)

        @block.gpsimd
        def _(pool):
            for cnt in BY_POOL:
                cnt.start(pool)

            def ln1_deviation(b):
                wait(pool, ln1_stats, b, 1)
                pool.tensor_tensor(rs1[:, :], vl1[:, :], power[:, :], ALU.pow).then_inc(ln1_power.sem, 1)
                wait(pool, ln1_power, b, 1)
                pool.tensor_tensor(nb1[:, :], nm1[:, :], rs1[:, :], ALU.mult).then_inc(ln1_dev.sem, 1)

            def deviation(b, c, var, mvs, rss, powered, done):
                q = c % 2
                wait(pool, var, b, c + 1)
                pool.tensor_tensor(rss[q][:, 0:1], mvs[q][:, 2:3], power[:, 0:1], ALU.pow).then_inc(powered.sem, 1)
                wait(pool, powered, b, c + 1)
                apart(pool)
                pool.tensor_scalar(rss[q][:, 1:2], mvs[q][:, 0:1], rss[q][:, 0:1], -1.0, ALU.mult, ALU.mult).then_inc(done.sem, 1)

            def masked_a(t, c):
                n = t.n
                wait(pool, dt_ready, n, 1)
                if t.mode != "pro1":
                    filled(pool, t, f"seg{c}")
                pool.tensor_tensor(arhs[c][:, :, :], LE.unsqueeze(1).broadcast_to([P, H, P]),
                                   da[n.par][:, c, :].unsqueeze(2).broadcast_to([P, H, P]), ALU.mult).then_inc(arhs_ready.sem, 1)

            def scale_B(t, c):
                b = t.b
                wait(pool, ec_ready, b, 1)
                if c == 0:
                    wait(pool, btok_ready, b, 1)
                else:
                    filled(pool, t, f"dS{c - 1}")
                pool.tensor_tensor(Bh[:, :, :], Btok[b.par][:, c, :].unsqueeze(1).broadcast_to([P, H, NS]),
                                   ec[:, 1, c, :].unsqueeze(2).broadcast_to([P, H, NS]), ALU.mult).then_inc(Bh_ready.sem, 1)

            def decay(t, c):
                filled(pool, t, f"yo{c}")
                pool.tensor_tensor(St[:, :, :], St[:, :, :], ec[0:NS, 2, c, :].unsqueeze(2).broadcast_to([NS, H, HD]),
                                   ALU.mult).then_inc(S_decayed.sem, 1)

            def modulate(t, c):
                b = t.b
                wait(pool, n2_ready, b, c + 1)
                pool.tensor_tensor(h2[:, c, :], n2[c % 2][:, :], mrow[b.par][:, 1, :], ALU.mult).then_inc(h2_scaled.sem, 1)
                wait(pool, h2_scaled, b, c + 1)
                pool.tensor_tensor(h2[:, c, :], h2[:, c, :], mrow[b.par][:, 2, :], ALU.add).then_inc(h2_ready.sem, 1)

            def pad_regions():
                pool.memset(padrow[:, :], 0.0).then_inc(setup_pool, 1)
                pool.wait_ge(setup_pool, 3)
                pool.memset(padrow[:, 3 * D:].bitcast(I32), 2 * TOK).then_inc(setup_pool, 1)
                pool.wait_ge(setup_pool, 4)
                pool.wait_ge(pad_ready, 1)
                for e in range(E):
                    pool.indirect_dma_start(out=slots, out_offset=bass.IndirectOffsetOnAxis(padi[:, e:e + 1], 0),
                                            in_=padrow[:, :], in_offset=None).then_inc(pad_stored, 16)

            def body(t):
                b = t.b
                n, m = t.projecting(1), t.projecting(2)
                pool.wait_ge(mod_loaded[b.par], b.i * 16 + 16)
                wait(pool, gab_ready, b, 1)
                scale_B(t, 0)
                pool.wait_ge(x_loaded[b.par], b.i * 16 + 16)
                pool.tensor_tensor(xin[b.par][:, :, :], xin[b.par][:, :, :], gab[:, :].unsqueeze(1).broadcast_to([P, NC, D]),
                                   ALU.add).then_inc(xg_ready.sem, 1)
                for s in range(NC):
                    if 0 < s < NC - 1:
                        decay(t, s)
                    if s > 1:
                        modulate(t, s - 2)
                    deviation(b, s, y_var, mvy, rs, y_power, y_stats)
                    if s < NC - 2:
                        scale_B(t, s + 1)
                    if s > 0:
                        deviation(b, s - 1, x1_var, mvx, rs2, x1_power, x1_stats)
                    if n:
                        if s > 0:
                            masked_a(n, s - 1)
                modulate(t, NC - 2)
                if m:
                    ln1_deviation(m.n)
                deviation(b, NC - 1, x1_var, mvx, rs2, x1_power, x1_stats)
                if n:
                    masked_a(n, NC - 1)
                modulate(t, NC - 1)
                wait(pool, gate_ready, b, 1)
                pool.tensor_tensor(rowbuf[:, :, 0:D], h2[:, :, :], mx[:, 3, :].unsqueeze(2).broadcast_to([P, NC, D]),
                                   ALU.mult).then_inc(h2g_ready.sem, 1)
                if t.mode == "last":
                    pad_regions()
                wait(pool, pos_ready, b, 1)
                wait(pool, gbrow_ready, b, 1)
                wait(pool, h2g_ready, b, 1)
                for c in range(NC):
                    wait(pool, base_ready, b, c + 1)
                    apart(pool)
                    pool.indirect_dma_start(out=slots, out_offset=bass.IndirectOffsetOnAxis(posi[:, c:c + 1], 0),
                                            in_=rowbuf[:, c, :], in_offset=None).then_inc(scattered, 16)

            pool.memset(rowbuf[:, 0, :], 0.0).then_inc(setup_pool, 1)
            pool.wait_ge(setup_pool, 1)
            pool.memset(rowbuf[:, 0, 3 * D:].bitcast(I32), 2 * TOK).then_inc(setup_pool, 1)
            pool.wait_ge(setup_pool, 2)
            pool.dma_start(slots[E * REG:, :], rowbuf[:, 0, :]).then_inc(scattered, 16)
            pool.memset(power[:, :], -0.5).then_inc(power_set, 1)
            pool.wait_ge(power_set, 1)
            ln1_deviation(FIRST)
            for c in range(NC):
                masked_a(PRO1.projecting(1), c)
            ln1_deviation(Batch(0, 1))
            turns(pool, body)
            routed_gpsimd(pool)


def kernel(**inputs):
    import numpy as np
    import concourse.bacc as bacc
    from concourse.bass_utils import run_bass_kernel_spmd as run

    g = {k: np.asarray(v) for k, v in inputs.items()}

    def tiles(w):
        return np.ascontiguousarray(w.reshape(-1, P, w.shape[-1]).transpose(1, 0, 2))

    def expert(gu, down):
        return np.concatenate([tiles(gu).reshape(P, -1), tiles(down).reshape(P, -1)], 1)

    cols = np.concatenate([
        g["L0_attn_conv_w"].reshape(NT, P, 4).transpose(1, 0, 2).reshape(P, -1),
        g["L0_attn_conv_b"].reshape(NT, P).T,
        g["L0_attn_in_proj_b"][DI:DI + NT * P].reshape(NT, P).T,
        g["L0_attn_ln_w"].reshape(KI, P).T, g["L0_attn_ln_b"].reshape(KI, P).T], 1)
    rows = np.concatenate([g["L0_attn_in_proj_b"][:DI], g["L0_attn_in_proj_b"][NPROJ - H:], g["L0_attn_dt_bias"],
                           g["L0_attn_A_log"], g["L0_attn_out_proj_b"]])
    k = np.zeros((P, NCONST), np.float32)
    r = np.arange(P)
    k[:, C_ID:C_ID + P] = r[:, None] == r
    k[:, C_LE:C_LE + P] = r[:, None] <= r
    k[:, C_GT:C_GT + P] = r[:, None] > r
    k[:, C_LT:C_LT + P] = r[:, None] < r
    k[:, C_ONE:C_ONE + P] = 1
    e, i = np.arange(E), np.arange(NBLK)
    k[:, C_TIE:C_TIE + E] = E - e
    k[:, C_REG:C_REG + E] = e * REG
    k[:, C_TID:C_TID + NC] = r[:, None] + P * np.arange(NC)
    k[:, C_P] = r
    k[:, C_CMP:C_CMP + TOK // P] = P * np.arange(TOK // P)
    k[:, C_I:C_I + NBLK] = i
    k[:, C_OFF:C_OFF + NBLK * E] = (i[:, None] * P + (e - E) * REG).reshape(-1)
    k[:, C_E:C_E + E] = e * WE
    arrays = {
        "u": g["L0_attn_u"],
        "w_in": tiles(g["L0_attn_in_proj_w"].T), "w_out": tiles(g["L0_attn_out_proj_w"].T),
        "w_router": tiles(g["L0_ffn_router_w"].T), "w_mod": tiles(g["L0_wmod"]), "c_t": tiles(g["L0_c"].T),
        "w_experts": np.stack([expert(a, b) for a, b in zip(g["L0_ffn_w_gate_up"], g["L0_ffn_w_down"])], 1),
        "w_shared": expert(g["L0_ffn_shared_gate_up"], g["L0_ffn_shared_down"]),
        "cols_in": cols, "rows_in": rows, "consts_in": k,
    }
    arrays = {n: np.ascontiguousarray(a) for n, a in arrays.items()}
    nc = bacc.Bacc("TRN2", target_bir_lowering=False, num_devices=1)
    args = [nc.dram_tensor(n, a.shape, mybir.dt.from_np(a.dtype), kind="ExternalInput").ap() for n, a in arrays.items()]
    args.append(nc.dram_tensor("result", (TOK, D), F32, kind="ExternalOutput").ap())
    build(nc, *args)
    r = run(nc, [arrays], core_ids=[0])
    return r.results[0]["result"].reshape(NB, SEQ, D)
```
